# Optimizing a Trainium2 kernel written in Bass

```python
import numpy as np
import jax
import jax.numpy as jnp

def _softmax(x, axis=-1):
    return jax.nn.softmax(x, axis=axis)

def _gelu(x):
    return jax.nn.gelu(x, approximate=True)

def _silu(x):
    return jax.nn.silu(x)

def _sigmoid(x):
    return jax.nn.sigmoid(x)

def _layernorm(x, axis=-1, eps=1e-05):
    m = jnp.mean(x, axis=axis, keepdims=True)
    v = jnp.var(x, axis=axis, keepdims=True)
    return (x - m) / jnp.sqrt(v + eps)

def _scatter_add(tgt, idx, src, axis=0):
    return tgt.at[idx].add(src)

def _segment_sum(src, seg, n):
    return jax.ops.segment_sum(src, seg, n)
kernel_name = 'mk_conv_preact_d1_conv_nchw128_r4_0f927a'

def setup_inputs(seed: int=0):
    np.random.seed(seed)
    _w = jnp.asarray

    def _rec_inputs():
        import jax
        import jax.numpy as jnp
        _gk = jax.random.key(seed)
        x = -0.0003929 + 0.9999 * jax.random.normal(jax.random.fold_in(_gk, 1), (2, 32, 64, 64), jnp.float32)
        return x
    x = _rec_inputs()

    def _L0_conv_setup():
        import jax, jax.numpy as jnp
        import numpy as np
        from jax import lax
        BN_EPS = 0.001
        BN_S = float(1.0 / np.sqrt(1.0 + BN_EPS))
        DN = ('NCHW', 'OIHW', 'NCHW')

        def conv3(x, w, stride):
            return lax.conv_general_dilated(x, w, (stride, stride), [(1, 1), (1, 1)], dimension_numbers=DN)

        def conv1x1(x, w, stride):
            return lax.conv_general_dilated(x, w, (stride, stride), [(0, 0), (0, 0)], dimension_numbers=DN)

        def deconv2(x, w):
            n, c, h, wd = x.shape
            y = jnp.einsum('nchw,cokl->nohkwl', x, w)
            return y.reshape(n, w.shape[1], 2 * h, 2 * wd)

        def basic_block(x, w1, w2, stride=1, ds=None):
            out = jax.nn.relu(conv3(x, w1, stride) * BN_S)
            out = conv3(out, w2, 1) * BN_S
            identity = conv1x1(x, ds, stride) * BN_S if ds is not None else x
            return jax.nn.relu(out + identity)
        key = jax.random.key(seed)
        ks = jax.random.split(key, 18)
        D = 32
        w33 = lambda k: jax.random.normal(k, (D, D, 3, 3), jnp.float32) * 0.04
        w11 = lambda k: jax.random.normal(k, (D, D, 1, 1), jnp.float32) * 0.12
        wT = lambda k: jax.random.normal(k, (D, D, 2, 2), jnp.float32) * 0.06
        return {'x': jax.random.normal(ks[0], (2, D, 64, 64), jnp.float32), 'e0b0c1': w33(ks[1]), 'e0b0c2': w33(ks[2]), 'e0b1c1': w33(ks[3]), 'e0b1c2': w33(ks[4]), 'e1b0c1': w33(ks[5]), 'e1b0c2': w33(ks[6]), 'e1b0ds': w11(ks[7]), 'e1b1c1': w33(ks[8]), 'e1b1c2': w33(ks[9]), 'e2b0c1': w33(ks[10]), 'e2b0c2': w33(ks[11]), 'e2b0ds': w11(ks[12]), 'e2b1c1': w33(ks[13]), 'e2b1c2': w33(ks[14]), 'dec0w': wT(ks[15]), 'dec1w': wT(ks[16])}
    _L0_conv_all = _L0_conv_setup()
    _L0_conv_in = {k: v for k, v in _L0_conv_all.items() if k in ('e0b0c1', 'e0b0c2', 'e0b1c1', 'e0b1c2', 'e1b0c1', 'e1b0c2', 'e1b0ds', 'e1b1c1', 'e1b1c2', 'e2b0c1', 'e2b0c2', 'e2b0ds', 'e2b1c1', 'e2b1c2', 'dec0w', 'dec1w')}
    del _L0_conv_all
    return {'x': x, 'L0_conv_e0b0c1': _L0_conv_in['e0b0c1'], 'L0_conv_e0b0c2': _L0_conv_in['e0b0c2'], 'L0_conv_e0b1c1': _L0_conv_in['e0b1c1'], 'L0_conv_e0b1c2': _L0_conv_in['e0b1c2'], 'L0_conv_e1b0c1': _L0_conv_in['e1b0c1'], 'L0_conv_e1b0c2': _L0_conv_in['e1b0c2'], 'L0_conv_e1b0ds': _L0_conv_in['e1b0ds'], 'L0_conv_e1b1c1': _L0_conv_in['e1b1c1'], 'L0_conv_e1b1c2': _L0_conv_in['e1b1c2'], 'L0_conv_e2b0c1': _L0_conv_in['e2b0c1'], 'L0_conv_e2b0c2': _L0_conv_in['e2b0c2'], 'L0_conv_e2b0ds': _L0_conv_in['e2b0ds'], 'L0_conv_e2b1c1': _L0_conv_in['e2b1c1'], 'L0_conv_e2b1c2': _L0_conv_in['e2b1c2'], 'L0_conv_dec0w': _L0_conv_in['dec0w'], 'L0_conv_dec1w': _L0_conv_in['dec1w']}

def reference(x, L0_conv_e0b0c1, L0_conv_e0b0c2, L0_conv_e0b1c1, L0_conv_e0b1c2, L0_conv_e1b0c1, L0_conv_e1b0c2, L0_conv_e1b0ds, L0_conv_e1b1c1, L0_conv_e1b1c2, L0_conv_e2b0c1, L0_conv_e2b0c2, L0_conv_e2b0ds, L0_conv_e2b1c1, L0_conv_e2b1c2, L0_conv_dec0w, L0_conv_dec1w):
    import jax
    import jax.numpy as jnp

    def _L0_conv_ref(x, e0b0c1, e0b0c2, e0b1c1, e0b1c2, e1b0c1, e1b0c2, e1b0ds, e1b1c1, e1b1c2, e2b0c1, e2b0c2, e2b0ds, e2b1c1, e2b1c2, dec0w, dec1w):
        import jax, jax.numpy as jnp
        import numpy as np
        from jax import lax
        BN_EPS = 0.001
        BN_S = float(1.0 / np.sqrt(1.0 + BN_EPS))
        DN = ('NCHW', 'OIHW', 'NCHW')

        def conv3(x, w, stride):
            return lax.conv_general_dilated(x, w, (stride, stride), [(1, 1), (1, 1)], dimension_numbers=DN)

        def conv1x1(x, w, stride):
            return lax.conv_general_dilated(x, w, (stride, stride), [(0, 0), (0, 0)], dimension_numbers=DN)

        def deconv2(x, w):
            n, c, h, wd = x.shape
            y = jnp.einsum('nchw,cokl->nohkwl', x, w)
            return y.reshape(n, w.shape[1], 2 * h, 2 * wd)

        def basic_block(x, w1, w2, stride=1, ds=None):
            out = jax.nn.relu(conv3(x, w1, stride) * BN_S)
            out = conv3(out, w2, 1) * BN_S
            identity = conv1x1(x, ds, stride) * BN_S if ds is not None else x
            return jax.nn.relu(out + identity)
        x = basic_block(x, e0b0c1, e0b0c2)
        x = basic_block(x, e0b1c1, e0b1c2)
        f0 = x
        x = basic_block(x, e1b0c1, e1b0c2, stride=2, ds=e1b0ds)
        x = basic_block(x, e1b1c1, e1b1c2)
        f1 = x
        x = basic_block(x, e2b0c1, e2b0c2, stride=2, ds=e2b0ds)
        x = basic_block(x, e2b1c1, e2b1c2)
        x = (jax.nn.relu(deconv2(x, dec0w) * BN_S) + f1) * BN_S
        x = (jax.nn.relu(deconv2(x, dec1w) * BN_S) + f0) * BN_S
        return x

    def _gn(v, G=32, eps=1e-05):
        B_, C_, H_, W_ = v.shape
        g = v.reshape(B_, G, C_ // G, H_, W_)
        m = jnp.mean(g, axis=(2, 3, 4), keepdims=True)
        s = jnp.var(g, axis=(2, 3, 4), keepdims=True)
        return ((g - m) / jnp.sqrt(s + eps)).reshape(v.shape)

    def _ln_c(v, eps=1e-06):
        m = jnp.mean(v, axis=1, keepdims=True)
        s = jnp.var(v, axis=1, keepdims=True)
        return (v - m) / jnp.sqrt(s + eps)

    def _ln_t(v, eps=1e-05):
        m = jnp.mean(v, axis=-1, keepdims=True)
        s = jnp.var(v, axis=-1, keepdims=True)
        return (v - m) / jnp.sqrt(s + eps)

    def _to_tokens(v):
        B_, C_, H_, W_ = v.shape
        return v.reshape(B_, C_, H_ * W_).transpose(0, 2, 1)

    def _from_tokens(t, like):
        B_, C_, H_, W_ = like.shape
        return t.transpose(0, 2, 1).reshape(B_, C_, H_, W_)
    x = x + _L0_conv_ref(_gn(x), L0_conv_e0b0c1, L0_conv_e0b0c2, L0_conv_e0b1c1, L0_conv_e0b1c2, L0_conv_e1b0c1, L0_conv_e1b0c2, L0_conv_e1b0ds, L0_conv_e1b1c1, L0_conv_e1b1c2, L0_conv_e2b0c1, L0_conv_e2b0c2, L0_conv_e2b0ds, L0_conv_e2b1c1, L0_conv_e2b1c2, L0_conv_dec0w, L0_conv_dec1w)
    return x

_drawn_inputs = setup_inputs


def setup_inputs(seed=0):
    import zlib

    import numpy as np

    out = dict(_drawn_inputs(seed))
    spreads = {}
    factors = {'L0_conv_e1b0c1': 3.184,
     'L0_conv_e1b0c2': 2.812,
     'L0_conv_e1b1c1': 4.951,
     'L0_conv_e1b1c2': 4.057,
     'L0_conv_e2b0c1': 8.0,
     'L0_conv_e2b0c2': 8.0,
     'L0_conv_e2b0ds': 8.0,
     'L0_conv_e2b1c1': 8.0,
     'L0_conv_e2b1c2': 8.0,
     'L0_conv_dec0w': 7.486}
    for name, (base, spread) in spreads.items():
        noise = np.random.default_rng([zlib.crc32(name.encode()), seed]).standard_normal(out[name].shape)
        drawn = base * np.exp(spread * noise) if base else spread * noise
        out[name] = jnp.asarray(drawn.astype(out[name].dtype))
    for name, factor in factors.items():
        out[name] = (out[name] * factor).astype(out[name].dtype)
    return out
```

```python
from contextlib import ExitStack

import concourse.bass as bass
from concourse import mybir

F32 = mybir.dt.float32
F32R = mybir.dt.float32r
ACT = mybir.ActivationFunctionType
ALU = mybir.AluOpType

IMAGES, CH, SIDE = 2, 32, 64
P = 4 * CH
BLOCKS = [SIDE // 2, SIDE // 4, SIDE // 8]
FRONT = [2, 2, 1]
EVEN_ROWS = [f + b + 1 for f, b in zip(FRONT, BLOCKS)]
EVEN_COLS = [38, 22, 12]
ODD_ROWS = [b + 1 for b in BLOCKS]
ODD_COLS = [b + 2 for b in BLOCKS]
BN_SCALE = float(1.0 / (1.0 + 0.001) ** 0.5)
GN_EPS = 1e-5
BANK = 512
BANKS = 8
STATS = 6
RAW_SLOTS = 4
RELU_SLOTS = 4

WEIGHTS = [
    ("e0b0c1", 4, BN_SCALE), ("e0b0c2", 4, BN_SCALE), ("e0b1c1", 4, BN_SCALE), ("e0b1c2", 4, BN_SCALE),
    ("e1b0c1", 9, BN_SCALE), ("e1b0c2", 4, BN_SCALE), ("e1b0ds", 4, BN_SCALE),
    ("e1b1c1", 4, BN_SCALE), ("e1b1c2", 4, BN_SCALE),
    ("e2b0c1", 9, BN_SCALE), ("e2b0c2", 4, BN_SCALE), ("e2b0ds", 4, BN_SCALE),
    ("e2b1c1", 4, BN_SCALE), ("e2b1c2", 4, BN_SCALE),
    ("dec0w", 4, BN_SCALE), ("dec1w", 4, BN_SCALE ** 3),
]
W_INDEX = {name: k for k, (name, _, _) in enumerate(WEIGHTS)}


class Stage:

    def __init__(self, name, kind, level, rows, residual=None, shortcut=None):
        self.name, self.kind, self.level, self.rows = name, kind, level, rows
        self.residual, self.shortcut = residual, shortcut
        if kind == "dec1":
            self.total = 2
            return
        self.total = ODD_ROWS[level] if kind in ("odd", "down") else BLOCKS[level]


STAGES = [
    Stage("e0b0c1", "odd", 0, 11),
    Stage("e0b0c2", "even", 0, 16, residual="normed"),
    Stage("e0b1c1", "odd", 0, 11),
    Stage("e0b1c2", "even", 0, 16, residual="block0"),
    Stage("e1b0c1", "down", 1, 17),
    Stage("e1b0c2", "even", 1, 16, shortcut="e1b0ds"),
    Stage("e1b1c1", "odd", 1, 17),
    Stage("e1b1c2", "even", 1, 16, shortcut="identity"),
    Stage("e2b0c1", "down", 2, 9),
    Stage("e2b0c2", "even", 2, 8, shortcut="e2b0ds"),
    Stage("e2b1c1", "odd", 2, 9),
    Stage("e2b1c2", "even", 2, 8, shortcut="identity"),
    Stage("dec0w", "dec0", 1, 16),
    Stage("dec1w", "dec1", 0, 1),
]


class Piece:
    def __init__(self, stage, index, image, row, rows):
        self.stage, self.index, self.image, self.row, self.rows = stage, index, image, row, rows


def cut_pieces():
    pieces = []
    for s, stage in enumerate(STAGES):
        for image in range(IMAGES):
            for row in range(0, stage.total, stage.rows):
                pieces.append(Piece(s, len(pieces), image, row, min(stage.rows, stage.total - row)))
    return pieces


PIECES = cut_pieces()
MAPPED = [p for p in PIECES if STAGES[p.stage].kind != "dec1"]
NORM_ROWS = 16
NORM_PIECES = BLOCKS[0] // NORM_ROWS


def produced(stage, image, last_row):
    done = [p.index for p in PIECES if p.stage == stage and p.image == image and p.row <= last_row]
    return max(done) + 1


def last_row_read(piece):
    stage = STAGES[piece.stage]
    end = piece.row + piece.rows - 1
    if stage.kind == "odd":
        return min(end, BLOCKS[stage.level] - 1)
    if stage.kind == "down":
        return min(2 * end, BLOCKS[stage.level - 1] - 1)
    if stage.kind == "even":
        return end + 1
    return BLOCKS[2] - 1 if stage.kind == "dec0" else BLOCKS[1] - 1


def build(nc, x, consts, weights, out):
    ctx = ExitStack()
    with ctx:
        def sb(name, shape, dt=F32):
            return ctx.enter_context(nc.sbuf_tensor(name, shape, dt))

        def sem(name):
            return ctx.enter_context(nc.semaphore(name))

        x_sb = sb("x_sb", [P, IMAGES, 32, 32])
        normed = sb("normed", [P, IMAGES, 32, 32])
        block0 = sb("block0", [P, IMAGES, 32, 32])
        skip0 = sb("skip0", [P, IMAGES, 32, 32])
        skip1 = sb("skip1", [P, IMAGES, 4, 8, 8])
        result = sb("result", [P, IMAGES, 4, 16, 16])
        even = [sb(f"even{v}", [P, 2, IMAGES, EVEN_ROWS[v], EVEN_COLS[v]], F32R) for v in range(3)]
        odd = [sb(f"odd{v}", [P, 2, IMAGES, ODD_ROWS[v], ODD_COLS[v]], F32R) for v in range(3)]
        up = sb("up", [P, 2, IMAGES, 16, 16], F32R)
        inside = [sb(f"inside{v}", [P, ODD_ROWS[v], ODD_COLS[v]]) for v in range(3)]
        relu = sb("relu", [P, RELU_SLOTS, BANK])
        raw = sb("raw", [P, RAW_SLOTS, 9, P])
        w_sb = [sb(f"w_{n}", [P, 2, m, P], F32R) for n, m, _ in WEIGHTS]
        const_sb = sb("const_sb", [P, 2 * P + 4])
        same_channel = const_sb[:, 0:P]
        eye = const_sb[:, P:2 * P]
        quad_mask = const_sb[:, 2 * P:2 * P + 4]
        eye_r = sb("eye_r", [P, P], F32R)
        stats = sb("stats", [P, IMAGES, NORM_PIECES, STATS])
        spread = sb("spread", [P, IMAGES, 4, NORM_PIECES * STATS])
        all_stats = sb("all_stats", [P, IMAGES, 4 * NORM_PIECES * STATS])
        moments = sb("moments", [P, IMAGES, 2])
        scratch = sb("scratch", [P, IMAGES, 8])
        psum = ctx.enter_context(nc.psum_tensor("psum", [P, BANKS, BANK], F32))

        const_loaded = sem("const_loaded")
        x_loaded = [[sem(f"x_loaded{i}_{h}") for h in range(NORM_PIECES)] for i in range(IMAGES)]
        w_loaded = [sem(f"w_loaded_{n}") for n, _, _ in WEIGHTS]
        zeros_set = sem("zeros_set")
        eye_ready = sem("eye_ready")
        norm_step = sem("norm_step")
        stats_spread = sem("stats_spread")
        stats_summed = sem("stats_summed")
        variance = sem("variance")
        deviation = sem("deviation")
        norm_ready = sem("norm_ready")
        norm_hi = sem("norm_hi")
        norm_lo = sem("norm_lo")
        w_hi = sem("w_hi")
        w_lo = sem("w_lo")
        summed = sem("summed")
        relu_ready = sem("relu_ready")
        hi_ready = sem("hi_ready")
        lo_ready = sem("lo_ready")
        lo_kept = sem("lo_kept")
        skip1_ready = sem("skip1_ready")
        skip0_scaled = sem("skip0_scaled")
        skip0_ready = sem("skip0_ready")
        stored = sem("stored")

        def even_inside(level, half, image, row, rows):
            f, b = FRONT[level], BLOCKS[level]
            return even[level][:, half, image, f + row:f + row + rows, f:f + b]

        def wait_lo(engine, index):
            kept = STAGES[PIECES[index].stage].residual is not None
            engine.wait_ge(lo_kept if kept else lo_ready,
                           sum((STAGES[p.stage].residual is not None) == kept for p in PIECES[:index + 1]))

        def bank_of(piece):
            return psum[:, piece.index % BANKS, :]

        def rows_of(flat, piece):
            stage = STAGES[piece.stage]
            cols = ODD_COLS[stage.level] if stage.kind in ("odd", "down") else BLOCKS[stage.level]
            return flat[:, 0:piece.rows * cols].rearrange("p (r c) -> p r c", c=cols)

        def quadrant_of(piece, j):
            return bank_of(piece)[:, 256 * j:256 * j + 256].rearrange("p (a b) -> p a b", a=16)

        def fp32_of(piece):
            stage = STAGES[piece.stage]
            if stage.residual is not None:
                return block0[:, piece.image, piece.row:piece.row + piece.rows, :]
            return rows_of(relu[:, piece.index % RELU_SLOTS, :], piece)

        def split_of(piece, half):
            stage = STAGES[piece.stage]
            if stage.kind in ("odd", "down"):
                return odd[stage.level][:, half, piece.image, piece.row:piece.row + piece.rows, :]
            return even_inside(stage.level, half, piece.image, piece.row, piece.rows)

        def dec0_parts(piece, half):
            flat = relu[:, piece.index % RELU_SLOTS, 0:256].rearrange("p (i j a b) -> p i a j b", i=2, j=2, a=8)
            home = up[:, half, piece.image, :, :].rearrange("p (a i) (b j) -> p i a j b", i=2, j=2)
            return [(flat[:, i], home[:, i]) for i in range(2)]

        block = ctx.enter_context(nc.Block())

        @block.sync
        def _(sp):
            def load_x(image):
                for h in range(NORM_PIECES):
                    rows = slice(h * NORM_ROWS, (h + 1) * NORM_ROWS)
                    sp.dma_start(x_sb[:, image, rows, :], x[:, image, rows, :]).then_inc(x_loaded[image][h], 16)

            load_x(0)
            sp.dma_start(const_sb[:], consts[:]).then_inc(const_loaded, 16)
            for k, (name, products, _) in enumerate(WEIGHTS):
                if k >= RAW_SLOTS:
                    sp.wait_ge(w_lo, k - RAW_SLOTS + 1)
                sp.dma_start(raw[:, k % RAW_SLOTS, 0:products, :], weights[k][:]).then_inc(w_loaded[k], 16)
                if k == 0:
                    load_x(1)
            for piece in PIECES[len(MAPPED):]:
                sp.wait_ge(relu_ready, piece.index + 1)
                quads = slice(2 * piece.row, 2 * piece.row + 2)
                sp.dma_start(out[:, piece.image, quads], result[:, piece.image, quads]).then_inc(stored, 16)
            sp.wait_ge(stored, 16 * (len(PIECES) - len(MAPPED)))

        @block.gpsimd
        def _(pool):
            for v in range(3):
                f, b = FRONT[v], BLOCKS[v]
                maps = even[v][:].bitcast(F32).rearrange("p h i r c -> p (h i) r c")
                pool.memset(maps[:, :, 0:f, :], 0.0)
                pool.memset(maps[:, :, f + b:, :], 0.0)
                pool.memset(maps[:, :, f:f + b, 0:f], 0.0)
                pool.memset(maps[:, :, f:f + b, f + b:], 0.0).then_inc(zeros_set, 1)

            for n in range(IMAGES * NORM_PIECES):
                image, row = n // NORM_PIECES, n % NORM_PIECES * NORM_ROWS
                pool.wait_ge(norm_hi, n + 1)
                pool.tensor_tensor(even_inside(0, 1, image, row, NORM_ROWS),
                                   normed[:, image, row:row + NORM_ROWS, :],
                                   even_inside(0, 0, image, row, NORM_ROWS).bitcast(F32),
                                   ALU.subtract).then_inc(norm_lo, 1)

            for piece in MAPPED:
                stage = STAGES[piece.stage]
                pool.wait_ge(hi_ready, piece.index + 1)
                if stage.kind == "dec0":
                    parts = [dec0_parts(piece, h) for h in range(2)]
                    for (flat, hi), (_, lo) in zip(*parts):
                        last = pool.tensor_tensor(lo, flat, hi.bitcast(F32), ALU.subtract)
                    last.then_inc(lo_ready, 1)
                elif stage.residual is None:
                    pool.tensor_tensor(split_of(piece, 1), fp32_of(piece), split_of(piece, 0).bitcast(F32),
                                       ALU.subtract).then_inc(lo_ready, 1)
                if stage.name == "e1b0c1":
                    pool.wait_ge(skip0_scaled, piece.image + 1)
                    pool.tensor_tensor(skip0[:, piece.image], skip0[:, piece.image], x_sb[:, piece.image],
                                       ALU.add).then_inc(skip0_ready, 1)
                if stage.name == "e1b1c2":
                    wait_lo(pool, piece.index)
                    hi = even_inside(1, 0, piece.image, 0, 16).bitcast(F32)
                    lo = even_inside(1, 1, piece.image, 0, 16).bitcast(F32)
                    for q in range(4):
                        i, j = q // 2, q % 2
                        last = pool.tensor_tensor(skip1[:, piece.image, q], hi[:, i::2, j::2], lo[:, i::2, j::2],
                                                  ALU.add)
                    last.then_inc(skip1_ready, 1)

        @block.scalar
        def _(act):
            def weights_hi(k):
                _, products, scale = WEIGHTS[k]
                act.wait_ge(w_loaded[k], 16)
                act.activation(w_sb[k][:, 0], raw[:, k % RAW_SLOTS, 0:products, :], ACT.Copy,
                               scale=scale).then_inc(w_hi, 1)

            act.wait_ge(const_loaded, 16)
            act.activation(eye_r[:], eye, ACT.Copy).then_inc(eye_ready, 1)
            for image in range(IMAGES):
                act.wait_ge(variance, image + 1)
                act.activation(scratch[:, image, 1:2], scratch[:, image, 0:1], ACT.Sqrt).then_inc(deviation, 1)
                if image == 0:
                    weights_hi(0)
                for h in range(NORM_PIECES):
                    row = h * NORM_ROWS
                    act.wait_ge(norm_ready, image * NORM_PIECES + h + 1)
                    if image == 0 and h == 0:
                        act.wait_ge(zeros_set, 3)
                    act.activation(even_inside(0, 0, image, row, NORM_ROWS),
                                   normed[:, image, row:row + NORM_ROWS, :], ACT.Copy).then_inc(norm_hi, 1)

            for piece in MAPPED:
                stage = STAGES[piece.stage]
                act.wait_ge(relu_ready, piece.index + 1)
                if stage.kind == "dec0":
                    for flat, hi in dec0_parts(piece, 0):
                        last = act.activation(hi, flat, ACT.Copy)
                    last.then_inc(hi_ready, 1)
                else:
                    act.activation(split_of(piece, 0), fp32_of(piece), ACT.Relu).then_inc(hi_ready, 1)
                if piece.index + 1 < len(WEIGHTS):
                    weights_hi(piece.index + 1)
                if stage.name == "e1b0c1":
                    act.activation(skip0[:, piece.image], block0[:, piece.image], ACT.Relu,
                                   scale=BN_SCALE).then_inc(skip0_scaled, 1)

        @block.vector
        def _(dve):
            steps = [0]

            def step(instruction):
                steps[0] += 1
                instruction.then_inc(norm_step, 1)
                dve.wait_ge(norm_step, steps[0])

            def weights_lo(k):
                _, products, scale = WEIGHTS[k]
                dve.wait_ge(w_hi, k + 1)
                dve.scalar_tensor_tensor(out=w_sb[k][:, 1], in0=raw[:, k % RAW_SLOTS, 0:products, :], scalar=scale,
                                         in1=w_sb[k][:, 0].bitcast(F32), op0=ALU.mult,
                                         op1=ALU.subtract).then_inc(w_lo, 1)

            def norm(image):
                for h in range(NORM_PIECES):
                    rows = slice(h * NORM_ROWS, (h + 1) * NORM_ROWS)
                    dve.wait_ge(x_loaded[image][h], 16)
                    last = dve.bn_stats(stats[:, image, h, :], x_sb[:, image, rows, :])
                step(last)
                if image == 0:
                    dve.wait_ge(const_loaded, 16)
                values = NORM_PIECES * STATS
                dve.tensor_tensor(spread[:, image],
                                  stats[:, image].rearrange("p h s -> p (h s)").unsqueeze(1)
                                  .to_broadcast([P, 4, values]),
                                  quad_mask.unsqueeze(2).to_broadcast([P, 4, values]),
                                  ALU.mult).then_inc(stats_spread, 1)
                dve.wait_ge(stats_summed, image + 1)
                step(dve.tensor_copy(all_stats[:, image], psum[:, BANKS - 1, 0:4 * values]))
                step(dve.bn_aggr(moments[:, image], all_stats[:, image]))
                s = scratch[:, image]
                dve.tensor_scalar(s[:, 0:1], moments[:, image, 1:2], GN_EPS, None, ALU.add).then_inc(variance, 1)
                dve.wait_ge(deviation, image + 1)
                step(dve.reciprocal(s[:, 2:3], s[:, 1:2]))
                step(dve.tensor_tensor(s[:, 3:4], s[:, 2:3], s[:, 2:3], ALU.mult))
                step(dve.tensor_tensor(s[:, 4:5], s[:, 3:4], s[:, 0:1], ALU.mult))
                step(dve.tensor_scalar(s[:, 5:6], s[:, 4:5], -0.5, 1.5, ALU.mult, ALU.add))
                step(dve.tensor_tensor(s[:, 6:7], s[:, 5:6], s[:, 2:3], ALU.mult))
                for h in range(NORM_PIECES):
                    rows = slice(h * NORM_ROWS, (h + 1) * NORM_ROWS)
                    dve.tensor_scalar(normed[:, image, rows, :], x_sb[:, image, rows, :], moments[:, image, 0:1],
                                      s[:, 6:7], ALU.subtract, ALU.mult).then_inc(norm_ready, 1)

            for v in range(3):
                last = dve.memset(inside[v][:], 1.0)
            step(last)
            for v in range(3):
                b = BLOCKS[v]
                dve.memset(inside[v][0:64, 0, 0:b + 1], 0.0)
                dve.memset(inside[v][64:128, b, 0:b + 1], 0.0)
                dve.memset(inside[v][:, :, b + 1:], 0.0)
                for i in range(2):
                    dve.memset(inside[v][64 * i:64 * i + 32, 1 - i:b + 1 - i, 0:1], 0.0)
                    last = dve.memset(inside[v][64 * i + 32:64 * i + 64, 1 - i:b + 1 - i, b:b + 1], 0.0)
            step(last)
            norm(0)
            weights_lo(0)
            norm(1)
            for piece in PIECES:
                stage = STAGES[piece.stage]
                image, rows = piece.image, slice(piece.row, piece.row + piece.rows)
                dve.wait_ge(summed, piece.index + 1)
                if stage.kind == "dec1":
                    if piece.index == len(MAPPED):
                        dve.wait_ge(skip0_ready, IMAGES)
                    for j in range(2):
                        last = dve.scalar_tensor_tensor(
                            out=result[:, image, 2 * piece.row + j], in0=quadrant_of(piece, j), scalar=0.0,
                            in1=skip0[:, image, piece.row::2, j::2], op0=ALU.max, op1=ALU.add)
                    last.then_inc(relu_ready, 1)
                    continue
                sums = rows_of(bank_of(piece), piece)
                if stage.residual is None and piece.index >= RELU_SLOTS:
                    wait_lo(dve, piece.index - RELU_SLOTS)
                if stage.kind in ("odd", "down"):
                    last = dve.scalar_tensor_tensor(out=fp32_of(piece), in0=sums, scalar=0.0,
                                                    in1=inside[stage.level][:, rows, :],
                                                    op0=ALU.max, op1=ALU.mult)
                elif stage.residual == "normed":
                    last = dve.tensor_tensor(fp32_of(piece), normed[:, image, rows, :], sums, ALU.add)
                elif stage.residual == "block0":
                    last = dve.scalar_tensor_tensor(out=fp32_of(piece), in0=block0[:, image, rows, :], scalar=0.0,
                                                    in1=sums, op0=ALU.max, op1=ALU.add)
                elif stage.kind == "even":
                    last = dve.tensor_scalar(fp32_of(piece), sums, 0.0, None, ALU.max)
                elif stage.kind == "dec0":
                    dve.wait_ge(skip1_ready, image + 1)
                    last = dve.scalar_tensor_tensor(out=relu[:, piece.index % RELU_SLOTS, 0:256],
                                                    in0=bank_of(piece)[:, 0:256], scalar=0.0,
                                                    in1=skip1[:, image].rearrange("p q a b -> p (q a b)"),
                                                    op0=ALU.max, op1=ALU.add)
                last.then_inc(relu_ready, 1)
                if 0 < piece.index < len(WEIGHTS):
                    weights_lo(piece.index)
                if stage.residual is not None:
                    dve.wait_ge(hi_ready, piece.index + 1)
                    dve.scalar_tensor_tensor(out=split_of(piece, 1), in0=fp32_of(piece), scalar=0.0,
                                             in1=split_of(piece, 0).bitcast(F32), op0=ALU.max,
                                             op1=ALU.subtract).then_inc(lo_kept, 1)

        @block.tensor
        def _(pe):
            def products(target, terms, first=True, final=True):
                for n, (w, moving) in enumerate(terms):
                    last = pe.matmul(target, w, moving, start=(first and n == 0),
                                     stop=(final and n == len(terms) - 1))
                return last

            def wait_source(piece, half):
                if piece.stage == 0:
                    pe.wait_ge(norm_lo if half else norm_hi,
                               piece.image * NORM_PIECES + last_row_read(piece) // NORM_ROWS + 1)
                elif half == 0:
                    pe.wait_ge(hi_ready, produced(piece.stage - 1, piece.image, last_row_read(piece)))
                else:
                    wait_lo(pe, produced(piece.stage - 1, piece.image, last_row_read(piece)) - 1)

            pe.wait_ge(const_loaded, 16)
            for image in range(IMAGES):
                pe.wait_ge(stats_spread, image + 1)
                if image == 1:
                    pe.wait_ge(variance, 1)
                pe.matmul(psum[:, BANKS - 1, 0:4 * NORM_PIECES * STATS], same_channel,
                          spread[:, image].rearrange("p q s -> p (q s)"),
                          start=True, stop=True).then_inc(stats_summed, 1)
            pe.wait_ge(eye_ready, 1)
            pe.wait_ge(zeros_set, 3)
            for piece in PIECES:
                stage = STAGES[piece.stage]
                w = w_sb[W_INDEX[stage.name]]
                image, level = piece.image, stage.level
                pe.wait_ge(w_lo, W_INDEX[stage.name] + 1)
                if piece.index >= BANKS:
                    pe.wait_ge(relu_ready, piece.index - BANKS + 1)
                if stage.kind == "dec0":
                    wait_source(piece, 1)
                    for q in range(4):
                        moving = [even_inside(2, half, image, 0, 8) for half in range(2)]
                        last = products(bank_of(piece)[:, 64 * q:64 * q + 64].rearrange("p (a b) -> p a b", a=8),
                                        [(w[:, 0, q], moving[0]), (w[:, 1, q], moving[0]), (w[:, 0, q], moving[1])])
                    last.then_inc(summed, 1)
                    continue
                if stage.kind == "dec1":
                    wait_source(piece, 1)
                    for j in range(2):
                        q = 2 * piece.row + j
                        moving = [up[:, half, image] for half in range(2)]
                        last = products(quadrant_of(piece, j),
                                        [(w[:, 0, q], moving[0]), (w[:, 1, q], moving[0]), (w[:, 0, q], moving[1])])
                    last.then_inc(summed, 1)
                    continue
                target = rows_of(bank_of(piece), piece)
                started = False
                if stage.shortcut == "identity":
                    products(target, [(eye_r[:], even_inside(level, half, image, piece.row, piece.rows))
                                      for half in range(2)], final=False)
                    started = True
                elif stage.shortcut is not None:
                    pe.wait_ge(w_lo, W_INDEX[stage.shortcut] + 1)
                    ds, f, b = w_sb[W_INDEX[stage.shortcut]], FRONT[level - 1], BLOCKS[level - 1]
                    terms = []
                    for q in range(4):
                        i, j = q // 2, q % 2
                        moving = [even[level - 1][:, half, image, f + i:f + b:2, f + j:f + b:2] for half in range(2)]
                        terms += [(ds[:, 0, q], moving[0]), (ds[:, 1, q], moving[0]), (ds[:, 0, q], moving[1])]
                    products(target, terms, final=False)
                    started = True

                if stage.kind == "even":
                    source, origin, stride, shifts, cols = odd[level], 0, 1, 2, BLOCKS[level]
                elif stage.kind == "odd":
                    source, origin, stride, shifts, cols = even[level], FRONT[level] - 1, 1, 2, ODD_COLS[level]
                else:
                    source, origin, stride, shifts, cols = even[level - 1], FRONT[level - 1] - 2, 2, 3, ODD_COLS[level]

                def moving(half, s):
                    r = origin + stride * piece.row + s // shifts
                    c = origin + s % shifts
                    return source[:, half, image, r:r + stride * (piece.rows - 1) + 1:stride,
                                  c:c + stride * (cols - 1) + 1:stride]

                wait_source(piece, 0)
                products(target, [(w[:, part, s], moving(0, s)) for part in range(2) for s in range(shifts ** 2)],
                         first=not started, final=False)
                wait_source(piece, 1)
                products(target, [(w[:, 0, s], moving(1, s)) for s in range(shifts ** 2)],
                         first=False).then_inc(summed, 1)


def blocks_of(image_map):
    n, c, h, w = image_map.shape
    return image_map.reshape(n, c, h // 2, 2, w // 2, 2).transpose(3, 5, 1, 0, 2, 4).reshape(4 * c, n, h // 2, w // 2)


def conv_blocks(w, stride):
    import numpy as np
    shifts = stride + 1
    packed = np.zeros((2, 2, w.shape[1], shifts, shifts, 2, 2, w.shape[0]), w.dtype)
    for i, s, o in np.ndindex(2, shifts, 2):
        dy = 2 * s + i - stride * o - (stride - 1)
        for j, t, p in np.ndindex(2, shifts, 2):
            dx = 2 * t + j - stride * p - (stride - 1)
            if 0 <= dy < 3 and 0 <= dx < 3:
                packed[i, j, :, s, t, o, p, :] = w[:, :, dy, dx].T
    return packed.reshape(4 * w.shape[1], shifts * shifts, 4 * w.shape[0])


def shortcut_blocks(w):
    import numpy as np
    packed = np.zeros((4, w.shape[1], 4, 4, w.shape[0]), w.dtype)
    for q in range(4):
        packed[0, :, q, q, :] = w[:, :, 0, 0].T
    return packed.reshape(4 * w.shape[1], 4, 4 * w.shape[0])


def deconv_blocks(w):
    import numpy as np
    packed = np.zeros((4, w.shape[0], 4, 4 * w.shape[1]), w.dtype)
    for q in range(4):
        packed[q, :, q, :] = w.transpose(0, 2, 3, 1).reshape(w.shape[0], -1)
    return packed.reshape(4 * w.shape[0], 4, 4 * w.shape[1])


def kernel(**inputs):
    import numpy as np
    import concourse.bacc as bacc
    from concourse.bass_utils import run_bass_kernel_spmd

    arrays = {"x_in": np.ascontiguousarray(blocks_of(np.asarray(inputs["x"])))}
    part = np.arange(P)
    consts = np.zeros((P, 2 * P + 4), np.float32)
    consts[:, 0:P] = part[:, None] % CH == part[None, :] % CH
    consts[:, P:2 * P] = part[:, None] == part[None, :]
    consts[:, 2 * P:] = part[:, None] // CH == np.arange(4)[None, :]
    arrays["consts_in"] = consts
    for name, _, _ in WEIGHTS:
        w = np.asarray(inputs["L0_conv_" + name])
        if name.startswith("dec"):
            packed = deconv_blocks(w)
        elif name.endswith("ds"):
            packed = shortcut_blocks(w)
        else:
            packed = conv_blocks(w, 2 if name in ("e1b0c1", "e2b0c1") else 1)
        arrays[name + "_in"] = np.ascontiguousarray(packed)

    nc = bacc.Bacc("TRN2", target_bir_lowering=False, num_devices=1)
    ap = {n: nc.dram_tensor(n, a.shape, F32, kind="ExternalInput").ap() for n, a in arrays.items()}
    out = nc.dram_tensor("out", (P, IMAGES, 4, 16, 16), F32, kind="ExternalOutput").ap()
    build(nc, ap["x_in"], ap["consts_in"], [ap[n + "_in"] for n, _, _ in WEIGHTS], out)
    got = run_bass_kernel_spmd(nc, [arrays], core_ids=[0]).results[0]["out"]
    got = got.reshape(2, 2, CH, IMAGES, 2, 2, 16, 16)
    return np.ascontiguousarray(got.transpose(3, 2, 6, 4, 0, 7, 5, 1).reshape(IMAGES, CH, SIDE, SIDE))
```

```python
from contextlib import ExitStack

import concourse.bass as bass
from concourse import mybir

F32 = mybir.dt.float32
F32R = mybir.dt.float32r
BF16 = mybir.dt.bfloat16
ACT = mybir.ActivationFunctionType
ALU = mybir.AluOpType

IMAGES, CH, SIDE = 2, 32, 64
P = 4 * CH
BLOCKS = [SIDE // 2, SIDE // 4, SIDE // 8]
FRONT = [2, 2, 1]
EVEN_ROWS = [f + b + 1 for f, b in zip(FRONT, BLOCKS)]
EVEN_COLS = [38, 22, 12]
ODD_ROWS = [b + 1 for b in BLOCKS]
ODD_COLS = [b + 2 for b in BLOCKS]
BN_SCALE = float(1.0 / (1.0 + 0.001) ** 0.5)
GN_EPS = 1e-5
BANK = 512
BANKS = 8
STATS = 6
STATS_ROWS = 16
STATS_PIECES = SIDE // 2 // STATS_ROWS
NORM_ROWS = [(0, 12), (12, 20)]
WARM_UP = [10, 8]
RAW_SLOTS = 4
RELU_SLOTS = 4

WEIGHTS = [
    ("e0b0c1", 4, BN_SCALE), ("e0b0c2", 4, BN_SCALE), ("e0b1c1", 4, BN_SCALE), ("e0b1c2", 4, BN_SCALE),
    ("e1b0c1", 9, BN_SCALE), ("e1b0c2", 4, BN_SCALE), ("e1b0ds", 1, BN_SCALE),
    ("e1b1c1", 4, BN_SCALE), ("e1b1c2", 4, BN_SCALE),
    ("e2b0c1", 9, BN_SCALE), ("e2b0c2", 4, BN_SCALE), ("e2b0ds", 1, BN_SCALE),
    ("e2b1c1", 4, BN_SCALE), ("e2b1c2", 4, BN_SCALE),
    ("dec0w", 4, BN_SCALE), ("dec1w", 4, BN_SCALE ** 3),
]
W_INDEX = {name: k for k, (name, _, _) in enumerate(WEIGHTS)}


class Stage:

    def __init__(self, name, kind, level, rows, residual=None, shortcut=None):
        self.name, self.kind, self.level, self.rows = name, kind, level, rows
        self.residual, self.shortcut = residual, shortcut
        self.together = level == 2 or kind == "dec0"
        self.direct = level > 0 and kind != "dec0"
        if kind == "dec1":
            self.total = 2
            return
        self.total = ODD_ROWS[level] if kind in ("odd", "down") else BLOCKS[level]


STAGES = [
    Stage("e0b0c1", "odd", 0, 11),
    Stage("e0b0c2", "even", 0, 16, residual="normed"),
    Stage("e0b1c1", "odd", 0, 11),
    Stage("e0b1c2", "even", 0, 16, residual="block0"),
    Stage("e1b0c1", "down", 1, 17),
    Stage("e1b0c2", "even", 1, 16, shortcut="e1b0ds"),
    Stage("e1b1c1", "odd", 1, 17),
    Stage("e1b1c2", "even", 1, 16, shortcut="identity"),
    Stage("e2b0c1", "down", 2, 9),
    Stage("e2b0c2", "even", 2, 8, shortcut="e2b0ds"),
    Stage("e2b1c1", "odd", 2, 9),
    Stage("e2b1c2", "even", 2, 8, shortcut="identity"),
    Stage("dec0w", "dec0", 1, 16),
    Stage("dec1w", "dec1", 0, 1),
]


class Piece:
    def __init__(self, stage, index, images, row, rows):
        self.stage, self.index, self.images, self.row, self.rows = stage, index, images, row, rows


def cut_pieces():
    pieces = []
    for s, stage in enumerate(STAGES):
        for images in [range(IMAGES)] if stage.together else [range(i, i + 1) for i in range(IMAGES)]:
            for row in range(0, stage.total, stage.rows):
                pieces.append(Piece(s, len(pieces), images, row, min(stage.rows, stage.total - row)))
    return pieces


PIECES = cut_pieces()


def last_piece(stage, images, last_row):
    return max(p.index for p in PIECES if p.stage == stage and p.images[0] <= images[-1]
               and images[0] <= p.images[-1] and p.row <= last_row)


def last_row_read(piece):
    stage = STAGES[piece.stage]
    end = piece.row + piece.rows - 1
    if stage.kind == "odd":
        return min(end, BLOCKS[stage.level] - 1)
    if stage.kind == "down":
        return min(2 * end, BLOCKS[stage.level - 1] - 1)
    return end + 1 if stage.kind == "even" else BLOCKS[2] - 1


def build(nc, x, consts, weights, out):
    ctx = ExitStack()
    with ctx:
        def sb(name, shape, dt=F32):
            return ctx.enter_context(nc.sbuf_tensor(name, shape, dt))

        def sem(name):
            return ctx.enter_context(nc.semaphore(name))

        x_sb = sb("x_sb", [P, IMAGES, 32, 32])
        normed = sb("normed", [P, IMAGES, 32, 32])
        block0 = sb("block0", [P, IMAGES, 32, 32])
        skip0 = sb("skip0", [P, IMAGES, 4, 4, 8, 8])
        skip1 = sb("skip1", [P, IMAGES, 4, 8, 8])
        result = sb("result", [P, IMAGES, 4, 4, 8, 8])
        even = [sb(f"even{v}", [P, 2, IMAGES, EVEN_ROWS[v], EVEN_COLS[v]], F32R) for v in range(3)]
        odd = [sb(f"odd{v}", [P, 2, IMAGES, ODD_ROWS[v], ODD_COLS[v]], F32R) for v in range(3)]
        up = sb("up", [P, 2, IMAGES, 4, 8, 8], F32R)
        corner = [sb(f"corner{v}", [P, 2, IMAGES, BLOCKS[v], BLOCKS[v]], F32R) for v in (1, 2)]
        inside = [sb(f"inside{v}", [P, IMAGES if v == 2 else 1, ODD_ROWS[v], ODD_COLS[v]]) for v in range(3)]
        zeros = sb("zeros", [P, BANK], BF16)
        relu = sb("relu", [P, RELU_SLOTS, BANK])
        raw = sb("raw", [P, RAW_SLOTS, 9, P])
        w_sb = [sb(f"w_{n}", [P, 2, m, P], F32R) for n, m, _ in WEIGHTS]
        same_channel = sb("same_channel", [P, P + 4])
        quad_mask = same_channel[:, P:P + 4]
        eye = sb("eye", [P, P])
        eye_r = sb("eye_r", [P, P], F32R)
        stats = sb("stats", [P, IMAGES, STATS_PIECES * STATS])
        spread = sb("spread", [P, IMAGES, 4, STATS_PIECES * STATS])
        moments = sb("moments", [P, IMAGES, 2])
        eps = sb("eps", [P, 2])
        scratch = sb("scratch", [P, IMAGES, 8])
        psum = ctx.enter_context(nc.psum_tensor("psum", [P, BANKS, BANK], F32))

        const_loaded = sem("const_loaded")
        eye_loaded = sem("eye_loaded")
        x_loaded = [[sem(f"x_loaded{i}_{h}") for h in range(STATS_PIECES)] for i in range(IMAGES)]
        w_loaded = [sem(f"w_loaded_{n}") for n, _, _ in WEIGHTS]
        zeros_set = sem("zeros_set")
        eye_ready = sem("eye_ready")
        ground_set = sem("ground_set")
        norm_step = sem("norm_step")
        stats_spread = sem("stats_spread")
        stats_summed = sem("stats_summed")
        moments_ready = sem("moments_ready")
        deviation = sem("deviation")
        scale_ready = sem("scale_ready")
        norm_ready = sem("norm_ready")
        norm_hi = sem("norm_hi")
        norm_lo = sem("norm_lo")
        w_hi = sem("w_hi")
        w_lo = sem("w_lo")
        summed = sem("summed")
        relu_ready = sem("relu_ready")
        hi_ready = sem("hi_ready")
        lo_ready = sem("lo_ready")
        lo_kept = sem("lo_kept")
        hi_direct = sem("hi_direct")
        lo_direct = sem("lo_direct")
        corner_ready = sem("corner_ready")
        up_sum = sem("up_sum")
        up_hi = sem("up_hi")
        up_lo = sem("up_lo")
        result_ready = sem("result_ready")
        skip1_ready = sem("skip1_ready")
        skip0_scaled = sem("skip0_scaled")
        skip0_added = sem("skip0_added")
        skip0_ready = sem("skip0_ready")
        stored = sem("stored")

        def even_inside(level, half, images, row, rows):
            f, b = FRONT[level], BLOCKS[level]
            at = even[level][:, half, images[0]:images[-1] + 1, f + row:f + row + rows, f:f + b]
            return at if len(images) > 1 else at[:, 0]

        def made_by(piece, half):
            stage = STAGES[piece.stage]
            if stage.direct:
                return lo_direct if half else hi_direct
            if half == 0:
                return hi_ready
            return lo_ready if stage.residual is None else lo_kept

        def wait_half(engine, index, half):
            signal = made_by(PIECES[index], half)
            engine.wait_ge(signal, sum(made_by(p, half) is signal for p in PIECES[:index + 1]))

        def bank_of(piece):
            return psum[:, piece.index % BANKS, :]

        def blocks_in(flat, piece):
            stage = STAGES[piece.stage]
            cols = ODD_COLS[stage.level] if stage.kind in ("odd", "down") else BLOCKS[stage.level]
            count = len(piece.images)
            if count == 1:
                return flat[:, 0:piece.rows * cols].rearrange("p (r c) -> p r c", c=cols)
            return flat[:, 0:count * piece.rows * cols].rearrange("p (i r c) -> p i r c", i=count, c=cols)

        def fp32_of(piece):
            if STAGES[piece.stage].residual is not None:
                return block0[:, piece.images[0], piece.row:piece.row + piece.rows, :]
            return blocks_in(relu[:, piece.index % RELU_SLOTS, :], piece)

        def split_of(piece, half):
            stage = STAGES[piece.stage]
            if stage.kind in ("odd", "down"):
                at = odd[stage.level][:, half, piece.images[0]:piece.images[-1] + 1,
                                      piece.row:piece.row + piece.rows, :]
                return at if len(piece.images) > 1 else at[:, 0]
            return even_inside(stage.level, half, piece.images, piece.row, piece.rows)

        def up32(image):
            return relu[:, DEC0.index % RELU_SLOTS, 256 * image:256 * image + 256]

        LEVEL0 = [p for p in PIECES if STAGES[p.stage].level == 0 and STAGES[p.stage].kind != "dec1"]
        LAST = [p for p in PIECES if STAGES[p.stage].kind == "dec1"]
        DEC0 = next(p for p in PIECES if STAGES[p.stage].kind == "dec0")
        last_of = {stage.name: last_piece(s, range(IMAGES), stage.total - 1) for s, stage in enumerate(STAGES)}

        block = ctx.enter_context(nc.Block())

        @block.sync
        def _(sp):
            def load_x(image):
                for h in range(STATS_PIECES):
                    rows = slice(h * STATS_ROWS, (h + 1) * STATS_ROWS)
                    sp.dma_start(x_sb[:, image, rows, :], x[:, image, rows, :]).then_inc(x_loaded[image][h], 16)

            load_x(0)
            sp.dma_start(same_channel[:], consts[:, 0:P + 4]).then_inc(const_loaded, 16)
            for k, (name, products, _) in enumerate(WEIGHTS):
                if k >= RAW_SLOTS:
                    sp.wait_ge(w_lo, k - RAW_SLOTS + 1)
                sp.dma_start(raw[:, k % RAW_SLOTS, 0:products, :], weights[k][:]).then_inc(w_loaded[k], 16)
                if k == 0:
                    load_x(1)
                if k == 1:
                    sp.dma_start(eye[:], consts[:, P + 4:]).then_inc(eye_loaded, 16)
            for n, piece in enumerate(LAST):
                sp.wait_ge(result_ready, n + 1)
                quads = slice(2 * piece.row, 2 * piece.row + 2)
                image = piece.images[0]
                sp.dma_start(out[:, image, quads], result[:, image, quads]).then_inc(stored, 16)
            sp.wait_ge(stored, 16 * len(LAST))

        @block.gpsimd
        def _(pool):
            for v in range(3):
                f, b = FRONT[v], BLOCKS[v]
                maps = even[v][:].bitcast(F32).rearrange("p h i r c -> p (h i) r c")
                pool.memset(maps[:, :, 0:f, :], 0.0)
                pool.memset(maps[:, :, f + b:, :], 0.0)
                pool.memset(maps[:, :, f:f + b, 0:f], 0.0)
                pool.memset(maps[:, :, f:f + b, f + b:], 0.0).then_inc(zeros_set, 1)

            for image in range(IMAGES):
                for n, (row, rows) in enumerate(NORM_ROWS):
                    done = image * len(NORM_ROWS) + n + 1
                    pool.wait_ge(norm_ready, done)
                    pool.wait_ge(norm_hi, done)
                    pool.tensor_tensor(even_inside(0, 1, [image], row, rows), normed[:, image, row:row + rows, :],
                                       even_inside(0, 0, [image], row, rows).bitcast(F32),
                                       ALU.subtract).then_inc(norm_lo, 1)

            for piece in LEVEL0:
                if STAGES[piece.stage].residual is None:
                    wait_half(pool, piece.index, 0)
                    pool.tensor_tensor(split_of(piece, 1), fp32_of(piece), split_of(piece, 0).bitcast(F32),
                                       ALU.subtract).then_inc(lo_ready, 1)

            for image in range(IMAGES):
                pool.wait_ge(skip0_scaled, image + 1)
                pool.tensor_tensor(normed[:, image], normed[:, image], x_sb[:, image], ALU.add).then_inc(skip0_added, 1)

            wait_half(pool, last_of["e1b1c2"], 1)
            for q in range(4):
                i, j = q // 2, q % 2
                hi, lo = [even_inside(1, half, range(IMAGES), 0, BLOCKS[1])[:, :, i::2, j::2].bitcast(F32)
                          for half in range(2)]
                last = pool.tensor_tensor(skip1[:, :, q], hi, lo, ALU.add)
            last.then_inc(skip1_ready, 1)

        @block.scalar
        def _(act):
            def weights_hi(k):
                _, products, scale = WEIGHTS[k]
                act.wait_ge(w_loaded[k], 16)
                act.activation(w_sb[k][:, 0], raw[:, k % RAW_SLOTS, 0:products, :], ACT.Copy,
                               scale=scale).then_inc(w_hi, 1)

            def gather_corners(level, images):
                f, b = FRONT[level - 1], BLOCKS[level - 1]
                for q in range(4):
                    i, j = q // 2, q % 2
                    source = even[level - 1][0:CH, :, images[0]:images[-1] + 1, f + i:f + b:2, f + j:f + b:2]
                    target = corner[level - 1][CH * q:CH * q + CH, :, images[0]:images[-1] + 1]
                    if len(images) > 1:
                        source, target = [t.rearrange("p h i r c -> p (h i) r c") for t in (source, target)]
                    else:
                        source, target = source[:, :, 0], target[:, :, 0]
                    last = act.activation(target, source.bitcast(F32), ACT.Copy)
                last.then_inc(corner_ready, 1)

            act.wait_ge(ground_set, 1)
            act.activation(scratch[:, 0, 7:8], eps[:, 0:1], ACT.Sqrt)
            weights_hi(0)
            for image in range(IMAGES):
                act.wait_ge(moments_ready, image + 1)
                act.activation(scratch[:, image, 0:1], moments[:, image, 1:2], ACT.Sqrt,
                               bias=eps[:, 0:1]).then_inc(deviation, 1)
                act.wait_ge(scale_ready, image + 1)
                if image == 0:
                    act.wait_ge(zeros_set, 3)
                for row, rows in NORM_ROWS:
                    act.activation(even_inside(0, 0, [image], row, rows), x_sb[:, image, row:row + rows, :],
                                   ACT.Identity, bias=scratch[:, image, 6:7],
                                   scale=scratch[:, image, 5:6]).then_inc(norm_hi, 1)
            act.wait_ge(eye_loaded, 16)
            act.activation(eye_r[:], eye[:], ACT.Copy).then_inc(eye_ready, 1)

            for piece in LEVEL0:
                act.wait_ge(relu_ready, piece.index + 1)
                act.activation(split_of(piece, 0), fp32_of(piece), ACT.Relu).then_inc(hi_ready, 1)
                if piece.index + 1 < len(WEIGHTS):
                    weights_hi(piece.index + 1)
            for image in range(IMAGES):
                wait_half(act, last_of["e0b1c2"], 1)
                gather_corners(1, [image])
            for image in range(IMAGES):
                act.activation(normed[:, image], block0[:, image], ACT.Relu, scale=BN_SCALE).then_inc(skip0_scaled, 1)
            wait_half(act, last_of["e1b1c2"], 1)
            gather_corners(2, range(IMAGES))
            for image in range(IMAGES):
                act.wait_ge(skip0_added, image + 1)
                for q in range(4):
                    for i in range(2):
                        row = 2 * i + q // 2
                        source = normed[:, image, row::4, q % 2::2].rearrange("p a (b j) -> p a j b", j=2)
                        target = skip0[:, image, q, 2 * i:2 * i + 2].rearrange("p j a b -> p a j b")
                        last = act.activation(target, source, ACT.Copy)
                last.then_inc(skip0_ready, 1)
            for image in range(IMAGES):
                act.wait_ge(up_sum, image + 1)
                act.activation(up[:, 0, image], up32(image), ACT.Copy).then_inc(up_hi, 1)

        @block.vector
        def _(dve):
            steps = [0]

            def step(instruction):
                steps[0] += 1
                instruction.then_inc(norm_step, 1)
                dve.wait_ge(norm_step, steps[0])

            def weights_lo(k):
                _, products, scale = WEIGHTS[k]
                dve.wait_ge(w_hi, k + 1)
                dve.scalar_tensor_tensor(out=w_sb[k][:, 1], in0=raw[:, k % RAW_SLOTS, 0:products, :], scalar=scale,
                                         in1=w_sb[k][:, 0].bitcast(F32), op0=ALU.mult,
                                         op1=ALU.subtract).then_inc(w_lo, 1)

            def norm(image):
                for h in range(STATS_PIECES):
                    rows = slice(h * STATS_ROWS, (h + 1) * STATS_ROWS)
                    dve.wait_ge(x_loaded[image][h], 16)
                    last = dve.bn_stats(stats[:, image, STATS * h:STATS * (h + 1)], x_sb[:, image, rows, :])
                step(last)
                values = STATS_PIECES * STATS
                if image == 0:
                    dve.wait_ge(const_loaded, 16)
                dve.tensor_tensor(spread[:, image], stats[:, image].unsqueeze(1).to_broadcast([P, 4, values]),
                                  quad_mask.unsqueeze(2).to_broadcast([P, 4, values]),
                                  ALU.mult).then_inc(stats_spread, 1)
                dve.wait_ge(stats_summed, image + 1)
                dve.bn_aggr(moments[:, image], psum[:, BANKS - 1, 0:4 * values]).then_inc(moments_ready, 1)
                mean, s = moments[:, image, 0:1], scratch[:, image]
                dve.wait_ge(moments_ready, image + 1)
                step(dve.tensor_scalar(s[:, 1:2], moments[:, image, 1:2], -1.0, -GN_EPS, ALU.mult, ALU.add))
                dve.wait_ge(deviation, image + 1)
                step(dve.reciprocal(s[:, 2:3], s[:, 0:1]))
                dve.tensor_scalar(s[:, 3:4], s[:, 2:3], 0.5, None, ALU.mult)
                step(dve.scalar_tensor_tensor(out=s[:, 4:5], in0=s[:, 2:3], scalar=s[:, 1:2], in1=s[:, 2:3],
                                              op0=ALU.mult, op1=ALU.mult))
                step(dve.scalar_tensor_tensor(out=s[:, 5:6], in0=s[:, 4:5], scalar=3.0, in1=s[:, 3:4],
                                              op0=ALU.add, op1=ALU.mult))
                dve.tensor_scalar(s[:, 6:7], s[:, 5:6], mean, -1.0, ALU.mult, ALU.mult).then_inc(scale_ready, 1)
                for n, (row, rows) in enumerate(NORM_ROWS):
                    dve.tensor_scalar(normed[:, image, row:row + rows, :], x_sb[:, image, row:row + rows, :], mean,
                                      s[:, 5:6], ALU.subtract, ALU.mult).then_inc(norm_ready, 1)
                    if image == 0 and n == 0:
                        weights_lo(0)

            dve.memset(zeros[:], 0.0)
            dve.memset(eps[:], GN_EPS).then_inc(ground_set, 1)
            for v in range(3):
                last = dve.memset(inside[v][:], 1.0)
            step(last)
            for v in range(3):
                b = BLOCKS[v]
                for m in range(IMAGES if v == 2 else 1):
                    mask = inside[v][:, m]
                    dve.memset(mask[0:64, 0, 0:b + 1], 0.0)
                    dve.memset(mask[64:128, b, 0:b + 1], 0.0)
                    dve.memset(mask[:, :, b + 1:], 0.0)
                    for i in range(2):
                        dve.memset(mask[64 * i:64 * i + 32, 1 - i:b + 1 - i, 0:1], 0.0)
                        last = dve.memset(mask[64 * i + 32:64 * i + 64, 1 - i:b + 1 - i, b:b + 1], 0.0)
            step(last)
            norm(0)
            norm(1)
            for piece in PIECES:
                stage = STAGES[piece.stage]
                image, rows = piece.images[0], slice(piece.row, piece.row + piece.rows)
                dve.wait_ge(summed, piece.index + 1)
                if stage.kind == "dec1":
                    if piece is LAST[0]:
                        dve.wait_ge(skip0_ready, IMAGES)
                    quads = slice(2 * piece.row, 2 * piece.row + 2)
                    dve.scalar_tensor_tensor(
                        out=result[:, image, quads].rearrange("p q s a b -> p (q s a b)"), in0=bank_of(piece),
                        scalar=0.0, in1=skip0[:, image, quads].rearrange("p q s a b -> p (q s a b)"),
                        op0=ALU.max, op1=ALU.add).then_inc(result_ready, 1)
                    continue
                if stage.kind == "dec0":
                    dve.wait_ge(skip1_ready, 1)
                    for image in range(IMAGES):
                        last = dve.scalar_tensor_tensor(
                            out=up32(image), in0=bank_of(piece)[:, 256 * image:256 * image + 256], scalar=0.0,
                            in1=skip1[:, image].rearrange("p q a b -> p (q a b)"), op0=ALU.max,
                            op1=ALU.add).then_inc(up_sum, 1)
                    for image in range(IMAGES):
                        dve.wait_ge(up_sum, image + 1)
                        dve.wait_ge(up_hi, image + 1)
                        last = dve.tensor_tensor(up[:, 1, image].rearrange("p q a b -> p (q a b)"), up32(image),
                                                 up[:, 0, image].rearrange("p q a b -> p (q a b)").bitcast(F32),
                                                 ALU.subtract).then_inc(up_lo, 1)
                    continue
                sums = blocks_in(bank_of(piece), piece)
                if stage.residual is None and piece.index >= RELU_SLOTS:
                    before = PIECES[piece.index - RELU_SLOTS]
                    wait_half(dve, before.index, 1)
                mask = inside[stage.level][:] if len(piece.images) > 1 else inside[stage.level][:, 0, rows, :]
                for target, signal in ([(split_of(piece, 0), hi_direct)] if stage.direct else []) + \
                        [(fp32_of(piece), relu_ready)]:
                    if stage.kind in ("odd", "down"):
                        last = dve.scalar_tensor_tensor(out=target, in0=sums, scalar=0.0, in1=mask,
                                                        op0=ALU.max, op1=ALU.mult)
                    elif stage.residual == "normed":
                        last = dve.tensor_tensor(target, normed[:, image, rows, :], sums, ALU.add)
                    elif stage.residual == "block0":
                        last = dve.scalar_tensor_tensor(out=target, in0=block0[:, image, rows, :], scalar=0.0,
                                                        in1=sums, op0=ALU.max, op1=ALU.add)
                    else:
                        last = dve.tensor_scalar(target, sums, 0.0, None, ALU.max)
                    last.then_inc(signal, 1)
                if 0 < piece.index < len(WEIGHTS):
                    weights_lo(piece.index)
                if stage.direct:
                    wait_half(dve, piece.index, 0)
                    dve.wait_ge(relu_ready, piece.index + 1)
                    dve.tensor_tensor(split_of(piece, 1), fp32_of(piece), split_of(piece, 0).bitcast(F32),
                                      ALU.subtract).then_inc(lo_direct, 1)
                elif stage.residual is not None:
                    wait_half(dve, piece.index, 0)
                    dve.scalar_tensor_tensor(out=split_of(piece, 1), in0=fp32_of(piece), scalar=0.0,
                                             in1=split_of(piece, 0).bitcast(F32), op0=ALU.max,
                                             op1=ALU.subtract).then_inc(lo_kept, 1)

        @block.tensor
        def _(pe):
            def products(target, terms, first=True, final=True):
                for n, (w, moving) in enumerate(terms):
                    last = pe.matmul(target, w, moving, start=(first and n == 0),
                                     stop=(final and n == len(terms) - 1))
                return last

            def wait_source(piece, half):
                last = last_row_read(piece)
                if piece.stage == 0:
                    pieces = sum(row <= last for row, _ in NORM_ROWS)
                    pe.wait_ge(norm_lo if half else norm_hi, piece.images[0] * len(NORM_ROWS) + pieces)
                else:
                    wait_half(pe, last_piece(piece.stage - 1, piece.images, last), half)

            def sum_stats(image):
                pe.wait_ge(stats_spread, image + 1)
                pe.matmul(psum[:, BANKS - 1, 0:4 * STATS_PIECES * STATS], same_channel[:, 0:P],
                          spread[:, image].rearrange("p q s -> p (q s)"),
                          start=True, stop=True).then_inc(stats_summed, 1)

            def warm_up(count):
                for _ in range(count):
                    pe.matmul(psum[:, BANKS - 2, :], zeros[:, 0:P], zeros[:], start=True, stop=True)

            pe.wait_ge(ground_set, 1)
            warm_up(WARM_UP[0])
            pe.wait_ge(const_loaded, 16)
            sum_stats(0)
            warm_up(WARM_UP[1])
            pe.wait_ge(zeros_set, 3)
            for piece in PIECES:
                stage = STAGES[piece.stage]
                k = W_INDEX[stage.name]
                w = w_sb[k]
                images, level = piece.images, stage.level
                at = slice(images[0], images[-1] + 1)
                if piece.index >= BANKS:
                    pe.wait_ge(relu_ready, piece.index - BANKS + 1)
                if stage.kind == "dec0":
                    pe.wait_ge(w_lo, k + 1)
                    targets = [bank_of(piece).rearrange("p (i q n) -> p i q n", i=IMAGES, q=4)[:, :, q]
                               .rearrange("p i (a b) -> p i a b", b=8) for q in range(4)]
                    hi, lo = [even_inside(2, half, images, 0, 8) for half in range(2)]
                    wait_source(piece, 0)
                    for q in range(4):
                        if q == 0:
                            wait_source(piece, 1)
                        last = products(targets[q], [(w[:, 0, q], hi), (w[:, 1, q], hi), (w[:, 0, q], lo)])
                    last.then_inc(summed, 1)
                    continue
                if stage.kind == "dec1":
                    pe.wait_ge(w_lo, k + 1)
                    pe.wait_ge(up_hi, images[0] + 1)
                    hi, lo = [up[:, half, images[0]].rearrange("p q a b -> p (q a b)") for half in range(2)]
                    for j in range(2):
                        q = 2 * piece.row + j
                        target = bank_of(piece)[:, 256 * j:256 * j + 256]
                        products(target, [(w[:, 0, q], hi), (w[:, 1, q], hi)], final=False)
                        pe.wait_ge(up_lo, images[0] + 1)
                        last = products(target, [(w[:, 0, q], lo)], first=False)
                    last.then_inc(summed, 1)
                    continue
                target = blocks_in(bank_of(piece), piece)
                terms = []
                if stage.shortcut == "identity":
                    if piece.row == 0 and level == 1:
                        pe.wait_ge(eye_ready, 1)
                    terms = [(eye_r[:], even_inside(level, half, images, piece.row, piece.rows)) for half in range(2)]
                elif stage.shortcut is not None:
                    pe.wait_ge(w_lo, W_INDEX[stage.shortcut] + 1)
                    pe.wait_ge(corner_ready, images[0] + 1 if level == 1 else IMAGES + 1)
                    ds = w_sb[W_INDEX[stage.shortcut]]
                    hi, lo = [corner[level - 1][:, half, at] for half in range(2)]
                    if len(images) == 1:
                        hi, lo = hi[:, 0], lo[:, 0]
                    terms = [(ds[:, 0, 0], hi), (ds[:, 1, 0], hi), (ds[:, 0, 0], lo)]
                started = len(terms) > 0
                if started:
                    products(target, terms, final=False)

                if stage.kind == "even":
                    source, origin, stride, shifts, cols = odd[level], 0, 1, 2, BLOCKS[level]
                elif stage.kind == "odd":
                    source, origin, stride, shifts, cols = even[level], FRONT[level] - 1, 1, 2, ODD_COLS[level]
                else:
                    source, origin, stride, shifts, cols = even[level - 1], FRONT[level - 1] - 2, 2, 3, ODD_COLS[level]

                def moving(half, s):
                    r = origin + stride * piece.row + s // shifts
                    c = origin + s % shifts
                    blocks = source[:, half, at, r:r + stride * (piece.rows - 1) + 1:stride,
                                    c:c + stride * (cols - 1) + 1:stride]
                    return blocks if len(images) > 1 else blocks[:, 0]

                pe.wait_ge(w_hi, k + 1)
                wait_source(piece, 0)
                products(target, [(w[:, 0, s], moving(0, s)) for s in range(shifts ** 2)],
                         first=not started, final=False)
                pe.wait_ge(w_lo, k + 1)
                products(target, [(w[:, 1, s], moving(0, s)) for s in range(shifts ** 2)],
                         first=False, final=False)
                wait_source(piece, 1)
                products(target, [(w[:, 0, s], moving(1, s)) for s in range(shifts ** 2)],
                         first=False).then_inc(summed, 1)
                if piece.index == 0:
                    sum_stats(1)


def blocks_of(image_map):
    n, c, h, w = image_map.shape
    return image_map.reshape(n, c, h // 2, 2, w // 2, 2).transpose(3, 5, 1, 0, 2, 4).reshape(4 * c, n, h // 2, w // 2)


def conv_blocks(w, stride):
    import numpy as np
    shifts = stride + 1
    packed = np.zeros((2, 2, w.shape[1], shifts, shifts, 2, 2, w.shape[0]), w.dtype)
    for i, s, o in np.ndindex(2, shifts, 2):
        dy = 2 * s + i - stride * o - (stride - 1)
        for j, t, p in np.ndindex(2, shifts, 2):
            dx = 2 * t + j - stride * p - (stride - 1)
            if 0 <= dy < 3 and 0 <= dx < 3:
                packed[i, j, :, s, t, o, p, :] = w[:, :, dy, dx].T
    return packed.reshape(4 * w.shape[1], shifts * shifts, 4 * w.shape[0])


def shortcut_blocks(w):
    import numpy as np
    packed = np.zeros((4, w.shape[1], 1, 4, w.shape[0]), w.dtype)
    for q in range(4):
        packed[q, :, 0, q, :] = w[:, :, 0, 0].T
    return packed.reshape(4 * w.shape[1], 1, 4 * w.shape[0])


def deconv_blocks(w):
    import numpy as np
    packed = np.zeros((4, w.shape[0], 4, 4 * w.shape[1]), w.dtype)
    for q in range(4):
        packed[q, :, q, :] = w.transpose(0, 2, 3, 1).reshape(w.shape[0], -1)
    return packed.reshape(4 * w.shape[0], 4, 4 * w.shape[1])


def kernel(**inputs):
    import numpy as np
    import concourse.bacc as bacc
    from concourse.bass_utils import run_bass_kernel_spmd

    arrays = {"x_in": np.ascontiguousarray(blocks_of(np.asarray(inputs["x"])))}
    part = np.arange(P)
    consts = np.zeros((P, 2 * P + 4), np.float32)
    consts[:, 0:P] = part[:, None] % CH == part[None, :] % CH
    consts[:, P:P + 4] = part[:, None] // CH == np.arange(4)[None, :]
    consts[:, P + 4:] = part[:, None] == part[None, :]
    arrays["consts_in"] = consts
    for name, _, _ in WEIGHTS:
        w = np.asarray(inputs["L0_conv_" + name])
        if name.startswith("dec"):
            packed = deconv_blocks(w)
        elif name.endswith("ds"):
            packed = shortcut_blocks(w)
        else:
            packed = conv_blocks(w, 2 if name in ("e1b0c1", "e2b0c1") else 1)
        arrays[name + "_in"] = np.ascontiguousarray(packed)

    nc = bacc.Bacc("TRN2", target_bir_lowering=False, num_devices=1)
    ap = {n: nc.dram_tensor(n, a.shape, F32, kind="ExternalInput").ap() for n, a in arrays.items()}
    out = nc.dram_tensor("out", (P, IMAGES, 4, 4, 8, 8), F32, kind="ExternalOutput").ap()
    build(nc, ap["x_in"], ap["consts_in"], [ap[n + "_in"] for n, _, _ in WEIGHTS], out)
    got = run_bass_kernel_spmd(nc, [arrays], core_ids=[0]).results[0]["out"]
    got = got.reshape(2, 2, CH, IMAGES, 2, 2, 2, 2, 8, 8)
    return np.ascontiguousarray(got.transpose(3, 2, 8, 6, 4, 0, 9, 7, 5, 1).reshape(IMAGES, CH, SIDE, SIDE))
```

```python
from contextlib import ExitStack

from concourse import mybir

F32 = mybir.dt.float32
F32R = mybir.dt.float32r
BF16 = mybir.dt.bfloat16
ACT = mybir.ActivationFunctionType
ALU = mybir.AluOpType

IMAGES, CH, SIDE = 2, 32, 64
P = 4 * CH
BLOCKS = [SIDE // 2, SIDE // 4, SIDE // 8]
FRONT = [2, 2, 1]
EVEN_ROWS = [f + b + 1 for f, b in zip(FRONT, BLOCKS)]
EVEN_COLS = [38, 22, 12]
ODD_ROWS = [b + 1 for b in BLOCKS]
ODD_COLS = [b + 2 for b in BLOCKS]
BN_SCALE = float(1.0 / (1.0 + 0.001) ** 0.5)
GN_EPS = 1e-5
BANK = 512
BANKS = 8
STATS = 6
STATS_ROWS = [(0, 10), (10, 12), (22, 10)]
VALUES = STATS * len(STATS_ROWS)
NORM_ROWS = [(0, 12), (12, 20)]
WARM_UP = [18, 11]
FILL = 2
LEAD = 1
LAST_ORDER = [(0, 0), (1, 0), (2, 0), (0, 1), (1, 1), (3, 0), (2, 1), (3, 1), (4, 0), (5, 0), (6, 0), (4, 1), (5, 1),
              (7, 0), (6, 1), (7, 1)]
RAW_SLOTS = 4
RELU_SLOTS = 4

WEIGHTS = [
    ("e0b0c1", 4, BN_SCALE), ("e0b0c2", 4, BN_SCALE), ("e0b1c1", 4, BN_SCALE), ("e0b1c2", 4, BN_SCALE),
    ("e1b0c1", 7, BN_SCALE), ("e1b0c2", 4, BN_SCALE), ("e1b0ds", 1, BN_SCALE),
    ("e1b1c1", 4, BN_SCALE), ("e1b1c2", 4, BN_SCALE),
    ("e2b0c1", 7, BN_SCALE), ("e2b0c2", 4, BN_SCALE), ("e2b0ds", 1, BN_SCALE),
    ("e2b1c1", 4, BN_SCALE), ("e2b1c2", 4, BN_SCALE),
    ("dec0w", 4, BN_SCALE), ("dec1w", 4, BN_SCALE ** 3),
]
STAGE_NAMES = [w[0] for w in WEIGHTS if not w[0].endswith("ds")]
STAGE = {name: s for s, name in enumerate(STAGE_NAMES)}
W_INDEX = {name: k for k, (name, _, _) in enumerate(WEIGHTS)}

WHOLE = [(1, 1), (1, 2), (2, 1), (2, 2), (0, 0)]
SIDES = [(0, 0, 2 * CH, 2 * CH, (0, 1)), (0, 2 * CH, 2 * CH, 2 * CH, (0, 2)),
         (1, 0, CH, CH, (1, 0)), (1, CH, 3 * CH, CH, (1, 0)),
         (1, 2 * CH, CH, CH, (2, 0)), (1, 3 * CH, 3 * CH, CH, (2, 0))]
SIDES_BY_ACT = {(1, 0): 2, (1, 1): 2, (2, 0): 3, (2, 1): 2}


class Stage:

    def __init__(self, name, kind, level, rows, residual=None, shortcut=None):
        self.name, self.kind, self.level, self.rows = name, kind, level, rows
        self.residual, self.shortcut = residual, shortcut
        self.together = level == 2 or kind in ("dec0", "dec1")
        self.direct = level > 0
        self.from_bank = self.direct and kind == "even"
        if kind in ("dec0", "dec1"):
            self.total = 2 if kind == "dec0" else 8
            return
        self.total = ODD_ROWS[level] if kind in ("odd", "down") else BLOCKS[level]


STAGES = [
    Stage("e0b0c1", "odd", 0, 11),
    Stage("e0b0c2", "even", 0, 16, residual="normed"),
    Stage("e0b1c1", "odd", 0, 11),
    Stage("e0b1c2", "even", 0, 16, residual="block0"),
    Stage("e1b0c1", "down", 1, 17),
    Stage("e1b0c2", "even", 1, 16, shortcut="e1b0ds"),
    Stage("e1b1c1", "odd", 1, 17),
    Stage("e1b1c2", "even", 1, 16, shortcut="identity"),
    Stage("e2b0c1", "down", 2, 9),
    Stage("e2b0c2", "even", 2, 8, shortcut="e2b0ds"),
    Stage("e2b1c1", "odd", 2, 9),
    Stage("e2b1c2", "even", 2, 8, shortcut="identity"),
    Stage("dec0w", "dec0", 1, 1),
    Stage("dec1w", "dec1", 0, 1),
]

RELU_WIDTH = STAGES[0].rows * ODD_COLS[0]


class Piece:
    def __init__(self, stage, index, images, row, rows):
        self.stage, self.index, self.images, self.row, self.rows = stage, index, images, row, rows


def cut_pieces():
    pieces = []
    for s, stage in enumerate(STAGES):
        for images in [range(IMAGES)] if stage.together else [range(i, i + 1) for i in range(IMAGES)]:
            for row in range(0, stage.total, stage.rows):
                pieces.append(Piece(s, len(pieces), images, row, min(stage.rows, stage.total - row)))
    return pieces


PIECES = cut_pieces()


def last_piece(stage, images, last_row):
    return max(p.index for p in PIECES if p.stage == stage and p.images[0] <= images[-1]
               and images[0] <= p.images[-1] and p.row <= last_row)


def last_row_read(piece):
    stage = STAGES[piece.stage]
    end = piece.row + piece.rows - 1
    if stage.kind == "odd":
        return min(end, BLOCKS[stage.level] - 1)
    if stage.kind == "down":
        return min(2 * end, BLOCKS[stage.level - 1] - 1)
    if stage.kind == "even":
        return end + 1
    return BLOCKS[2] - 1 if stage.kind == "dec0" else piece.row // 4


def build(nc, x, consts, weights, out):
    ctx = ExitStack()
    with ctx:
        def sb(name, shape, dt=F32):
            return ctx.enter_context(nc.sbuf_tensor(name, shape, dt))

        def sem(name):
            return ctx.enter_context(nc.semaphore(name))

        x_sb = sb("x_sb", [P, IMAGES, 32, 32])
        normed = sb("normed", [P, IMAGES, 32, 32])
        block0 = sb("block0", [P, IMAGES, 32, 32])
        skip0 = sb("skip0", [P, 8, IMAGES, 2, 8, 8])
        skip1 = sb("skip1", [P, 2, IMAGES, 2, 8, 8])
        result = sb("result", [P, 8, IMAGES * 2 * 64])
        even = [sb(f"even{v}", [P, 2, IMAGES, EVEN_ROWS[v], EVEN_COLS[v]], F32R) for v in range(3)]
        odd = [sb(f"odd{v}", [P, 2, IMAGES, ODD_ROWS[v], ODD_COLS[v]], F32R) for v in range(3)]
        corner = [sb(f"corner{v}", [P, 2, IMAGES, BLOCKS[v], BLOCKS[v]], F32R) for v in (1, 2)]
        sides_1 = sb("sides", [P, 2, 2, IMAGES, ODD_ROWS[1], ODD_COLS[1]], F32R)
        sides_flat = sides_1[:].rearrange("p s h i r c -> p (s h i r c)")[:, 0:8 * ODD_ROWS[2] * ODD_COLS[2]]
        sides = [None, sides_1, sides_flat.rearrange("p (s h i r c) -> p s h i r c", s=2, h=2, i=IMAGES,
                                                     r=ODD_ROWS[2])]
        up = corner[0][:].rearrange("p h i r c -> p h (i r c)").rearrange("p h (q n) -> p h q n", q=2)
        inside = [sb(f"inside{v}", [P, IMAGES if v == 2 else 1, ODD_ROWS[v], ODD_COLS[v]]) for v in range(3)]
        zeros = sb("zeros", [P, BANK // 2], BF16)
        relu = sb("relu", [P, RELU_SLOTS, RELU_WIDTH])
        raw = sb("raw", [P, RAW_SLOTS, max(m for _, m, _ in WEIGHTS), P])
        w_sb = [sb(f"w_{n}", [P, 2, m, P], F32R) for n, m, _ in WEIGHTS]
        same_channel = sb("same_channel", [P, P + 4])
        quad_mask = same_channel[:, P:P + 4]
        eye_r = sb("eye_r", [P, P], F32R)
        stats = sb("stats", [P, IMAGES, VALUES])
        moments = sb("moments", [P, IMAGES, 2])
        eps4 = sb("eps4", [P, 2])
        scratch = sb("scratch", [P, IMAGES, 8])
        psum = ctx.enter_context(nc.psum_tensor("psum", [P, BANKS, BANK], F32))

        const_loaded = sem("const_loaded")
        eye_loaded = sem("eye_loaded")
        x_loaded = [[sem(f"x_loaded{i}_{h}") for h in range(len(STATS_ROWS))] for i in range(IMAGES)]
        w_loaded = [sem(f"w_loaded_{n}") for n, _, _ in WEIGHTS]
        zeros_set = sem("zeros_set")
        eye_ready = sem("eye_ready")
        ground_set = sem("ground_set")
        norm_step = sem("norm_step")
        stats_spread = sem("stats_spread")
        stats_summed = sem("stats_summed")
        moments_ready = sem("moments_ready")
        deviation = sem("deviation")
        scale_ready = sem("scale_ready")
        norm_ready = sem("norm_ready")
        norm_hi_first = sem("norm_hi_first")
        norm_hi = sem("norm_hi")
        norm_lo_first = sem("norm_lo_first")
        norm_lo = sem("norm_lo")
        w_hi = sem("w_hi")
        w_scaled = sem("w_scaled")
        w_lo_first = sem("w_lo_first")
        w_lo = sem("w_lo")
        summed = sem("summed")
        relu_ready = sem("relu_ready")
        hi_ready = sem("hi_ready")
        lo_ready = sem("lo_ready")
        lo_kept = sem("lo_kept")
        hi_direct = sem("hi_direct")
        lo_direct = sem("lo_direct")
        up_lo_second = sem("up_lo_second")
        sides_by_act = sem("sides_by_act")
        sides_by_dve = sem("sides_by_dve")
        corner_ready = sem("corner_ready")
        skip1_ready = sem("skip1_ready")
        skip0_scaled = sem("skip0_scaled")
        skip0_added = sem("skip0_added")
        skip0_ready = sem("skip0_ready")
        result_ready = sem("result_ready")
        stored = sem("stored")

        def wait_w_lo(engine, k):
            if k == 0:
                engine.wait_ge(w_lo_first, 2)
            else:
                engine.wait_ge(w_lo, k)

        def even_inside(level, half, images, row, rows):
            f, b = FRONT[level], BLOCKS[level]
            at = even[level][:, half, images[0]:images[-1] + 1, f + row:f + row + rows, f:f + b]
            return at if len(images) > 1 else at[:, 0]

        def made_by(piece, half):
            stage = STAGES[piece.stage]
            if piece is DEC0[1] and half:
                return up_lo_second
            if stage.direct:
                return lo_direct if half else hi_direct
            if half == 0:
                return hi_ready
            return lo_ready if stage.residual is None else lo_kept

        def wait_half(engine, index, half):
            signal = made_by(PIECES[index], half)
            engine.wait_ge(signal, sum(made_by(p, half) is signal for p in PIECES[:index + 1]))

        def wait_relu(engine, index):
            if STAGES[PIECES[index].stage].from_bank:
                wait_half(engine, index, 1)
            else:
                engine.wait_ge(relu_ready, sum(not STAGES[p.stage].from_bank for p in PIECES[:index + 1]))

        def bank_of(piece):
            return psum[:, piece.index % BANKS, :]

        def blocks_in(flat, piece):
            stage = STAGES[piece.stage]
            cols = ODD_COLS[stage.level] if stage.kind in ("odd", "down") else BLOCKS[stage.level]
            count = len(piece.images)
            if count == 1:
                return flat[:, 0:piece.rows * cols].rearrange("p (r c) -> p r c", c=cols)
            return flat[:, 0:count * piece.rows * cols].rearrange("p (i r c) -> p i r c", i=count, c=cols)

        def fp32_of(piece):
            if STAGES[piece.stage].kind == "dec0":
                return relu[:, piece.index % RELU_SLOTS, 0:256]
            if STAGES[piece.stage].residual is not None:
                return block0[:, piece.images[0], piece.row:piece.row + piece.rows, :]
            return blocks_in(relu[:, piece.index % RELU_SLOTS, :], piece)

        def split_of(piece, half):
            stage = STAGES[piece.stage]
            if stage.kind == "dec0":
                return up[:, half, piece.row]
            if stage.kind in ("odd", "down"):
                at = odd[stage.level][:, half, piece.images[0]:piece.images[-1] + 1,
                                      piece.row:piece.row + piece.rows, :]
                return at if len(piece.images) > 1 else at[:, 0]
            return even_inside(stage.level, half, piece.images, piece.row, piece.rows)

        def up_lo(engine, piece, signal):
            wait_relu(engine, piece.index)
            wait_half(engine, piece.index, 0)
            engine.tensor_tensor(split_of(piece, 1), fp32_of(piece), split_of(piece, 0).bitcast(F32),
                                 ALU.subtract).then_inc(signal, 1)

        def side_copy(level, image, copy):
            side, to, start, count, (sy, sx) = copy
            f = FRONT[level - 1] - 2
            source = even[level - 1][start:start + count, :, image, f + sy:f + sy + 2 * ODD_ROWS[level] - 1:2,
                                     f + sx:f + sx + 2 * ODD_COLS[level] - 1:2]
            return sides[level][to:to + count, side, :, image], source.bitcast(F32)

        def source_of_level(level, image):
            return last_piece(STAGE["e0b1c2" if level == 1 else "e1b1c2"], [image], BLOCKS[level - 1] - 1)

        LEVEL0 = [p for p in PIECES if STAGES[p.stage].level == 0 and STAGES[p.stage].kind != "dec1"]
        LAST = [p for p in PIECES if STAGES[p.stage].kind == "dec1"]
        DEC0 = [p for p in PIECES if STAGES[p.stage].kind == "dec0"]

        spare = result[:].rearrange("p n c -> p (n c)")
        scaled = spare[:, 0:4 * P].rearrange("p (m c) -> p m c", m=4)
        eye = spare[:, 4 * P:5 * P]
        spread = spare[:, 5 * P:5 * P + IMAGES * 4 * VALUES].rearrange("p (i q s) -> p i q s", i=IMAGES, q=4)

        block = ctx.enter_context(nc.Block())

        @block.sync
        def _(sp):
            def load_x(image):
                for n, (row, rows) in enumerate(STATS_ROWS):
                    sp.dma_start(x_sb[:, image, row:row + rows, :],
                                 x[:, image, row:row + rows, :]).then_inc(x_loaded[image][n], 16)

            load_x(0)
            sp.dma_start(same_channel[:], consts[:, 0:P + 4]).then_inc(const_loaded, 16)
            for k, (name, products, _) in enumerate(WEIGHTS):
                if k >= RAW_SLOTS:
                    wait_w_lo(sp, k - RAW_SLOTS)
                sp.dma_start(raw[:, k % RAW_SLOTS, 0:products, :], weights[k][:]).then_inc(w_loaded[k], 16)
                if k == 0:
                    load_x(1)
                if k == 1:
                    sp.dma_start(eye, consts[:, P + 4:]).then_inc(eye_loaded, 16)
            stores = [(0, 1), (1, 1), (2, 2), (4, 2), (6, 2)]
            for first, count in stores:
                sp.wait_ge(result_ready, first + count)
                sp.dma_start(out[:, first:first + count], result[:, first:first + count]).then_inc(stored, 16)
            sp.wait_ge(stored, 16 * len(stores))

        @block.gpsimd
        def _(pool):
            for v in range(3):
                f, b = FRONT[v], BLOCKS[v]
                maps = even[v][:].bitcast(F32).rearrange("p h i r c -> p (h i) r c")
                pool.memset(maps[:, :, 0:f, :], 0.0)
                pool.memset(maps[:, :, f + b:, :], 0.0)
                pool.memset(maps[:, :, f:f + b, 0:f], 0.0)
                pool.memset(maps[:, :, f:f + b, f + b:], 0.0).then_inc(zeros_set, 1)

            pool.wait_ge(w_scaled, 1)
            pool.wait_ge(w_hi, 1)
            for half in range(2):
                at = slice(2 * half, 2 * half + 2)
                pool.tensor_tensor(w_sb[0][:, 1, at], scaled[:, at], w_sb[0][:, 0, at].bitcast(F32),
                                   ALU.subtract).then_inc(w_lo_first, 1)

            for image in range(IMAGES):
                row, rows = NORM_ROWS[1]
                pool.wait_ge(norm_ready, (image + 1) * len(NORM_ROWS))
                pool.wait_ge(norm_hi, image + 1)
                pool.tensor_tensor(even_inside(0, 1, [image], row, rows), normed[:, image, row:row + rows, :],
                                   even_inside(0, 0, [image], row, rows).bitcast(F32),
                                   ALU.subtract).then_inc(norm_lo, 1)

            for piece in LEVEL0:
                if STAGES[piece.stage].residual is None:
                    wait_half(pool, piece.index, 0)
                    pool.tensor_tensor(split_of(piece, 1), fp32_of(piece), split_of(piece, 0).bitcast(F32),
                                       ALU.subtract).then_inc(lo_ready, 1)

            for image in range(IMAGES):
                pool.wait_ge(skip0_scaled, image + 1)
                pool.tensor_tensor(normed[:, image], normed[:, image], x_sb[:, image], ALU.add).then_inc(skip0_added, 1)

            wait_half(pool, source_of_level(2, IMAGES - 1), 1)
            for q in range(4):
                i, j = q // 2, q % 2
                hi, lo = [even_inside(1, half, range(IMAGES), 0, BLOCKS[1])[:, :, i::2, j::2].bitcast(F32)
                          for half in range(2)]
                last = pool.tensor_tensor(skip1[:, i, :, j], hi, lo, ALU.add)
            last.then_inc(skip1_ready, 1)

            up_lo(pool, DEC0[1], up_lo_second)

        @block.scalar
        def _(act):
            def weights_hi(k):
                _, products, scale = WEIGHTS[k]
                act.wait_ge(w_loaded[k], 16)
                act.activation(w_sb[k][:, 0], raw[:, k % RAW_SLOTS, 0:products, :], ACT.Copy,
                               scale=scale).then_inc(w_hi, 1)

            def gather_corners(level, image, quadrants=range(4)):
                f, b = FRONT[level - 1], BLOCKS[level - 1]
                for q in quadrants:
                    i, j = q // 2, q % 2
                    source = even[level - 1][0:CH, :, image, f + i:f + b:2, f + j:f + b:2]
                    target = corner[level - 1][CH * q:CH * q + CH, :, image]
                    last = act.activation(target, source.bitcast(F32), ACT.Copy)
                if quadrants[-1] == 3:
                    last.then_inc(corner_ready, 1)

            def gather_sides(level, image):
                wait_half(act, source_of_level(level, image), 1)
                for copy in SIDES[:SIDES_BY_ACT[level, image]]:
                    target, source = side_copy(level, image, copy)
                    last = act.activation(target, source, ACT.Copy)
                last.then_inc(sides_by_act, 1)

            act.wait_ge(ground_set, 1)
            act.activation(scratch[:, 0, 7:8], eps4[:, 0:1], ACT.Sqrt)
            weights_hi(0)
            for image in range(IMAGES):
                act.wait_ge(moments_ready, image + 1)
                act.activation(scratch[:, image, 0:1], moments[:, image, 1:2], ACT.Sqrt,
                               bias=eps4[:, 0:1], scale=4.0).then_inc(deviation, 1)
                if image == 0:
                    act.activation(scaled, raw[:, 0, 0:4, :], ACT.Copy, scale=BN_SCALE).then_inc(w_scaled, 1)
                act.wait_ge(scale_ready, image + 1)
                if image == 0:
                    act.wait_ge(zeros_set, 3)
                row, rows = NORM_ROWS[1]
                act.activation(even_inside(0, 0, [image], row, rows), x_sb[:, image, row:row + rows, :],
                               ACT.Identity, bias=scratch[:, image, 6:7],
                               scale=scratch[:, image, 5:6]).then_inc(norm_hi, 1)
            act.wait_ge(eye_loaded, 16)
            act.activation(eye_r[:], eye, ACT.Copy).then_inc(eye_ready, 1)

            for piece in LEVEL0:
                wait_relu(act, piece.index)
                act.activation(split_of(piece, 0), fp32_of(piece), ACT.Relu).then_inc(hi_ready, 1)
                if piece.index + 1 < len(WEIGHTS):
                    weights_hi(piece.index + 1)
                if piece is LEVEL0[-3]:
                    gather_sides(1, 0)
                    gather_corners(1, 0, range(0, 2))
                if piece is LEVEL0[-2]:
                    gather_corners(1, 0, range(2, 4))
            gather_sides(1, 1)
            gather_corners(1, 1)
            for image in range(IMAGES):
                act.activation(normed[:, image], block0[:, image], ACT.Relu, scale=BN_SCALE).then_inc(skip0_scaled, 1)
            for image in range(IMAGES):
                gather_sides(2, image)
                gather_corners(2, image)
            for image in range(IMAGES):
                act.wait_ge(skip0_added, image + 1)
                for q in range(4):
                    for i in range(2):
                        row = 2 * i + q // 2
                        source = normed[:, image, row::4, q % 2::2].rearrange("p a (b j) -> p a j b", j=2)
                        target = skip0[:, 4 * i + q, image].rearrange("p j a b -> p a j b")
                        last = act.activation(target, source, ACT.Copy)
                last.then_inc(skip0_ready, 1)

        @block.vector
        def _(dve):
            steps = [0]

            def step(instruction):
                steps[0] += 1
                instruction.then_inc(norm_step, 1)
                dve.wait_ge(norm_step, steps[0])

            def weights_lo(k):
                _, products, scale = WEIGHTS[k]
                dve.wait_ge(w_hi, k + 1)
                dve.scalar_tensor_tensor(out=w_sb[k][:, 1], in0=raw[:, k % RAW_SLOTS, 0:products, :], scalar=scale,
                                         in1=w_sb[k][:, 0].bitcast(F32), op0=ALU.mult,
                                         op1=ALU.subtract).then_inc(w_lo, 1)

            def norm(image):
                for n, (row, rows) in enumerate(STATS_ROWS):
                    dve.wait_ge(x_loaded[image][n], 16)
                    last = dve.bn_stats(stats[:, image, STATS * n:STATS * (n + 1)], x_sb[:, image, row:row + rows, :])
                step(last)
                if image == 0:
                    dve.wait_ge(const_loaded, 16)
                dve.tensor_tensor(spread[:, image], stats[:, image].unsqueeze(1).to_broadcast([P, 4, VALUES]),
                                  quad_mask.unsqueeze(2).to_broadcast([P, 4, VALUES]),
                                  ALU.mult).then_inc(stats_spread, 1)
                dve.wait_ge(stats_summed, image + 1)
                dve.bn_aggr(moments[:, image], psum[:, BANKS - 1, 0:4 * VALUES]).then_inc(moments_ready, 1)
                mean, s = moments[:, image, 0:1], scratch[:, image]
                dve.wait_ge(moments_ready, image + 1)
                step(dve.tensor_scalar(s[:, 1:2], moments[:, image, 1:2], 4.0, 4.0 * GN_EPS, ALU.mult, ALU.add))
                dve.reciprocal(s[:, 3:4], s[:, 1:2]).then_inc(norm_step, 1)
                steps[0] += 1
                dve.wait_ge(deviation, image + 1)
                step(dve.reciprocal(s[:, 2:3], s[:, 0:1]))
                step(dve.scalar_tensor_tensor(out=s[:, 5:6], in0=s[:, 3:4], scalar=s[:, 0:1], in1=s[:, 2:3],
                                              op0=ALU.mult, op1=ALU.add))
                if image == 0:
                    dve.wait_ge(zeros_set, 1)
                row, rows = NORM_ROWS[0]
                dve.tensor_scalar(even_inside(0, 0, [image], row, rows), x_sb[:, image, row:row + rows, :], mean,
                                  s[:, 5:6], ALU.subtract, ALU.mult).then_inc(norm_hi_first, 1)
                dve.tensor_scalar(s[:, 6:7], s[:, 5:6], mean, -1.0, ALU.mult, ALU.mult).then_inc(scale_ready, 1)
                for n, (row, rows) in enumerate(NORM_ROWS):
                    dve.tensor_scalar(normed[:, image, row:row + rows, :], x_sb[:, image, row:row + rows, :], mean,
                                      s[:, 5:6], ALU.subtract, ALU.mult).then_inc(norm_ready, 1)
                    if n == 0:
                        dve.wait_ge(norm_ready, image * len(NORM_ROWS) + 1)
                        dve.wait_ge(norm_hi_first, image + 1)
                        dve.tensor_tensor(even_inside(0, 1, [image], row, rows), normed[:, image, row:row + rows, :],
                                          even_inside(0, 0, [image], row, rows).bitcast(F32),
                                          ALU.subtract).then_inc(norm_lo_first, 1)

            dve.memset(zeros[:], 0.0)
            dve.memset(eps4[:], 4.0 * GN_EPS).then_inc(ground_set, 1)

            def masks(levels):
                for v in levels:
                    last = dve.memset(inside[v][:], 1.0)
                step(last)
                for v in levels:
                    b = BLOCKS[v]
                    for m in range(IMAGES if v == 2 else 1):
                        mask = inside[v][:, m]
                        dve.memset(mask[0:64, 0, 0:b + 1], 0.0)
                        dve.memset(mask[64:128, b, 0:b + 1], 0.0)
                        dve.memset(mask[:, :, b + 1:], 0.0)
                        for i in range(2):
                            dve.memset(mask[64 * i:64 * i + 32, 1 - i:b + 1 - i, 0:1], 0.0)
                            last = dve.memset(mask[64 * i + 32:64 * i + 64, 1 - i:b + 1 - i, b:b + 1], 0.0)
                step(last)

            masks([0])
            norm(0)
            norm(1)
            masks([1, 2])
            for piece in PIECES[:DEC0[0].index]:
                stage = STAGES[piece.stage]
                image, rows = piece.images[0], slice(piece.row, piece.row + piece.rows)
                dve.wait_ge(summed, piece.index + 1)
                sums = blocks_in(bank_of(piece), piece)
                if stage.residual is None and not stage.from_bank and piece.index >= RELU_SLOTS:
                    before = PIECES[piece.index - RELU_SLOTS]
                    wait_half(dve, before.index, 1)
                if stage.kind in ("odd", "down"):
                    mask = inside[stage.level][:] if len(piece.images) > 1 else inside[stage.level][:, 0, rows, :]
                for target, signal in ([(split_of(piece, 0), hi_direct)] if stage.direct else []) + \
                        ([] if stage.from_bank else [(fp32_of(piece), relu_ready)]):
                    if stage.kind in ("odd", "down"):
                        last = dve.scalar_tensor_tensor(out=target, in0=sums, scalar=0.0, in1=mask,
                                                        op0=ALU.max, op1=ALU.mult)
                    elif stage.residual == "normed":
                        last = dve.tensor_tensor(target, normed[:, image, rows, :], sums, ALU.add)
                    elif stage.residual == "block0":
                        last = dve.scalar_tensor_tensor(out=target, in0=block0[:, image, rows, :], scalar=0.0,
                                                        in1=sums, op0=ALU.max, op1=ALU.add)
                    else:
                        last = dve.tensor_scalar(target, sums, 0.0, None, ALU.max)
                    last.then_inc(signal, 1)
                if 0 < piece.index < len(WEIGHTS):
                    weights_lo(piece.index)
                if stage.direct:
                    if not stage.from_bank:
                        wait_relu(dve, piece.index)
                    wait_half(dve, piece.index, 0)
                    lo, hi = split_of(piece, 1), split_of(piece, 0).bitcast(F32)
                    if stage.from_bank:
                        for one in range(len(piece.images)) if len(piece.images) > 1 else [slice(None)]:
                            last = dve.scalar_tensor_tensor(out=lo[:, one], in0=sums[:, one], scalar=0.0,
                                                            in1=hi[:, one], op0=ALU.max, op1=ALU.subtract)
                        last.then_inc(lo_direct, 1)
                    else:
                        dve.tensor_tensor(lo, fp32_of(piece), hi, ALU.subtract).then_inc(lo_direct, 1)
                elif stage.residual is not None:
                    wait_half(dve, piece.index, 0)
                    dve.scalar_tensor_tensor(out=split_of(piece, 1), in0=fp32_of(piece), scalar=0.0,
                                             in1=split_of(piece, 0).bitcast(F32), op0=ALU.max,
                                             op1=ALU.subtract).then_inc(lo_kept, 1)
                if piece.index in (source_of_level(level, image) for level in (1, 2)):
                    wait_half(dve, piece.index, 1)
                    for copy in SIDES[SIDES_BY_ACT[stage.level + 1, image]:]:
                        last = dve.tensor_copy(*side_copy(stage.level + 1, image, copy))
                    last.then_inc(sides_by_dve, 1)

            for piece in DEC0:
                dve.wait_ge(summed, piece.index + 1)
                dve.wait_ge(skip1_ready, 1)
                wait_half(dve, piece.index - RELU_SLOTS, 1)
                for target, signal in [(split_of(piece, 0), hi_direct), (fp32_of(piece), relu_ready)]:
                    dve.scalar_tensor_tensor(out=target, in0=bank_of(piece)[:, 0:256], scalar=0.0,
                                             in1=skip1[:, piece.row].rearrange("p i j a b -> p (i j a b)"),
                                             op0=ALU.max, op1=ALU.add).then_inc(signal, 1)
                if piece.row == 0:
                    up_lo(dve, piece, lo_direct)

            dve.wait_ge(skip0_ready, IMAGES)
            for piece in LAST:
                dve.wait_ge(summed, piece.index + 1)
                dve.scalar_tensor_tensor(out=result[:, piece.row], in0=bank_of(piece)[:, 0:256], scalar=0.0,
                                         in1=skip0[:, piece.row].rearrange("p i j a b -> p (i j a b)"),
                                         op0=ALU.max, op1=ALU.add).then_inc(result_ready, 1)

        @block.tensor
        def _(pe):
            def products(target, terms, first=True, final=True):
                for n, (w, moving) in enumerate(terms):
                    last = pe.matmul(target, w, moving, start=(first and n == 0),
                                     stop=(final and n == len(terms) - 1))
                return last

            def wait_source(piece, half):
                last = last_row_read(piece)
                if piece.stage == 0:
                    second = last >= NORM_ROWS[1][0]
                    pe.wait_ge(norm_lo_first if half else norm_hi_first, piece.images[0] + 1)
                    if second:
                        pe.wait_ge(norm_lo if half else norm_hi, piece.images[0] + 1)
                else:
                    wait_half(pe, last_piece(piece.stage - 1, piece.images, last), half)

            def sum_stats(image):
                pe.wait_ge(stats_spread, image + 1)
                pe.matmul(psum[:, BANKS - 1, 0:4 * VALUES], same_channel[:, 0:P],
                          spread[:, image].rearrange("p q s -> p (q s)"),
                          start=True, stop=True).then_inc(stats_summed, 1)

            def warm_up(count, bank=BANKS - 2):
                for _ in range(count):
                    pe.matmul(psum[:, bank, 0:256], zeros[:, 0:P], zeros[:, 0:256], start=True, stop=True)

            pe.wait_ge(ground_set, 1)
            warm_up(WARM_UP[0])
            sum_stats(0)
            warm_up(WARM_UP[1])
            pe.wait_ge(zeros_set, 3)
            for piece in PIECES[:DEC0[0].index]:
                stage = STAGES[piece.stage]
                k = W_INDEX[stage.name]
                w = w_sb[k]
                images, level = piece.images, stage.level
                at = slice(images[0], images[-1] + 1)
                if piece.index >= BANKS:
                    wait_relu(pe, piece.index - BANKS)
                target = blocks_in(bank_of(piece), piece)
                terms = []
                if stage.shortcut == "identity":
                    if piece.row == 0 and level == 1:
                        pe.wait_ge(eye_ready, 1)
                    terms = [(eye_r[:], even_inside(level, half, images, piece.row, piece.rows)) for half in range(2)]
                elif stage.shortcut is not None:
                    wait_w_lo(pe, W_INDEX[stage.shortcut])
                    pe.wait_ge(corner_ready, (level - 1) * IMAGES + images[-1] + 1)
                    ds = w_sb[W_INDEX[stage.shortcut]]
                    hi, lo = [corner[level - 1][:, half, at] for half in range(2)]
                    if len(images) == 1:
                        hi, lo = hi[:, 0], lo[:, 0]
                    terms = [(ds[:, 0, 0], hi), (ds[:, 1, 0], hi), (ds[:, 0, 0], lo)]
                started = len(terms) > 0
                if started:
                    products(target, terms, final=False)

                if stage.kind == "even":
                    source, origin, stride, shifts, cols = odd[level], 0, 1, 2, BLOCKS[level]
                elif stage.kind == "odd":
                    source, origin, stride, shifts, cols = even[level], FRONT[level] - 1, 1, 2, ODD_COLS[level]
                else:
                    source, origin, stride, shifts, cols = even[level - 1], FRONT[level - 1] - 2, 2, 3, ODD_COLS[level]

                def moving(half, s):
                    r = origin + stride * piece.row + s // shifts
                    c = origin + s % shifts
                    blocks = source[:, half, at, r:r + stride * (piece.rows - 1) + 1:stride,
                                    c:c + stride * (cols - 1) + 1:stride]
                    return blocks if len(images) > 1 else blocks[:, 0]

                pe.wait_ge(w_hi, k + 1)
                if level == 2:
                    wait_relu(pe, piece.index + 1 - BANKS)
                    warm_up(FILL, (piece.index + 1) % BANKS)
                if stage.kind == "down":
                    wait_source(piece, 0)
                    wait_w_lo(pe, k)
                    whole = [[moving(half, shifts * sy + sx) for sy, sx in WHOLE] for half in range(2)]
                    products(target, [(w[:, part, n], m) for part in range(2) for n, m in enumerate(whole[0])],
                             final=False)
                    wait_source(piece, 1)
                    products(target, [(w[:, 0, n], m) for n, m in enumerate(whole[1])], first=False, final=False)
                    pe.wait_ge(sides_by_act, (level - 1) * IMAGES + images[-1] + 1)
                    pe.wait_ge(sides_by_dve, (level - 1) * IMAGES + images[-1] + 1)
                    terms = []
                    for side in range(2):
                        hi, lo = [sides[level][:, side, half, at] for half in range(2)]
                        if len(images) == 1:
                            hi, lo = hi[:, 0], lo[:, 0]
                        n = len(WHOLE) + side
                        terms += [(w[:, 0, n], hi), (w[:, 1, n], hi), (w[:, 0, n], lo)]
                    products(target, terms, first=False).then_inc(summed, 1)
                    continue
                wait_source(piece, 0)
                products(target, [(w[:, 0, s], moving(0, s)) for s in range(shifts ** 2)],
                         first=not started, final=False)
                if piece.index == 0:
                    pe.wait_ge(w_lo_first, 1)
                    products(target, [(w[:, 1, s], moving(0, s)) for s in range(2)], first=False, final=False)
                    pe.wait_ge(w_lo_first, 2)
                    products(target, [(w[:, 1, s], moving(0, s)) for s in range(2, 4)], first=False, final=False)
                else:
                    wait_w_lo(pe, k)
                    products(target, [(w[:, 1, s], moving(0, s)) for s in range(shifts ** 2)],
                             first=False, final=False)
                if piece.index == 1:
                    sum_stats(1)
                wait_source(piece, 1)
                products(target, [(w[:, 0, s], moving(1, s)) for s in range(shifts ** 2)],
                         first=False).then_inc(summed, 1)

            w = w_sb[W_INDEX["dec0w"]]
            hi, lo = [even_inside(2, half, range(IMAGES), 0, BLOCKS[2]) for half in range(2)]
            groups = [(piece, j) for piece in DEC0 for j in range(2)]

            def dec0_target(piece, j):
                return bank_of(piece)[:, 0:256].rearrange("p (i j a b) -> p i j a b", i=IMAGES, j=2, a=8)[:, :, j]

            wait_w_lo(pe, W_INDEX["dec0w"])
            wait_relu(pe, DEC0[0].index - BANKS)
            warm_up(FILL, DEC0[0].index % BANKS)
            wait_source(DEC0[0], 0)
            for n in range(len(groups) + LEAD):
                if n < len(groups):
                    piece, j = groups[n]
                    q = 2 * piece.row + j
                    if j == 0:
                        wait_relu(pe, piece.index - BANKS)
                    pe.matmul(dec0_target(piece, j), w[:, 0, q], hi, start=(j == 0), stop=False,
                              skip_group_check=True)
                    pe.matmul(dec0_target(piece, j), w[:, 1, q], hi, start=False, stop=False,
                              skip_group_check=True)
                if n >= LEAD:
                    piece, j = groups[n - LEAD]
                    if n == LEAD:
                        wait_source(piece, 1)
                    last = pe.matmul(dec0_target(piece, j), w[:, 0, 2 * piece.row + j], lo, start=False, stop=(j == 1),
                                     skip_group_check=True)
                    if j == 1:
                        last.then_inc(summed, 1)

            w = w_sb[W_INDEX["dec1w"]]
            wait_w_lo(pe, W_INDEX["dec1w"])
            wait_relu(pe, LAST[0].index - BANKS)
            warm_up(FILL, LAST[0].index % BANKS)
            for n, half in LAST_ORDER:
                piece = LAST[n]
                source, q = up[:, half, piece.row // 4], piece.row % 4
                wait_source(piece, half)
                if half == 0:
                    wait_relu(pe, piece.index - BANKS)
                    products(bank_of(piece)[:, 0:256], [(w[:, part, q], source) for part in range(2)], final=False)
                else:
                    products(bank_of(piece)[:, 0:256], [(w[:, 0, q], source)], first=False).then_inc(summed, 1)


def blocks_of(image_map):
    n, c, h, w = image_map.shape
    return image_map.reshape(n, c, h // 2, 2, w // 2, 2).transpose(3, 5, 1, 0, 2, 4).reshape(4 * c, n, h // 2, w // 2)


def conv_blocks(w, stride):
    import numpy as np
    shifts = stride + 1
    packed = np.zeros((2, 2, w.shape[1], shifts, shifts, 2, 2, w.shape[0]), w.dtype)
    for i, s, o in np.ndindex(2, shifts, 2):
        dy = 2 * s + i - stride * o - (stride - 1)
        for j, t, p in np.ndindex(2, shifts, 2):
            dx = 2 * t + j - stride * p - (stride - 1)
            if 0 <= dy < 3 and 0 <= dx < 3:
                packed[i, j, :, s, t, o, p, :] = w[:, :, dy, dx].T
    return packed.reshape(4 * w.shape[1], shifts * shifts, 4 * w.shape[0])


def pack_sides(packed):
    import numpy as np
    whole = [packed[:, 3 * sy + sx] for sy, sx in WHOLE]
    pairs = np.zeros((P, 2, P), packed.dtype)
    for side, to, start, count, (sy, sx) in SIDES:
        pairs[to:to + count, side] = packed[start:start + count, 3 * sy + sx]
    return np.concatenate([np.stack(whole, 1), pairs], 1)


def shortcut_blocks(w):
    import numpy as np
    packed = np.zeros((4, w.shape[1], 1, 4, w.shape[0]), w.dtype)
    for q in range(4):
        packed[q, :, 0, q, :] = w[:, :, 0, 0].T
    return packed.reshape(4 * w.shape[1], 1, 4 * w.shape[0])


def deconv_blocks(w):
    import numpy as np
    packed = np.zeros((4, w.shape[0], 4, 4 * w.shape[1]), w.dtype)
    for q in range(4):
        packed[q, :, q, :] = w.transpose(0, 2, 3, 1).reshape(w.shape[0], -1)
    return packed.reshape(4 * w.shape[0], 4, 4 * w.shape[1])


def kernel(**inputs):
    import numpy as np
    import concourse.bacc as bacc
    from concourse.bass_utils import run_bass_kernel_spmd

    arrays = {"x_in": np.ascontiguousarray(blocks_of(np.asarray(inputs["x"])))}
    part = np.arange(P)
    consts = np.zeros((P, 2 * P + 4), np.float32)
    consts[:, 0:P] = part[:, None] % CH == part[None, :] % CH
    consts[:, P:P + 4] = part[:, None] // CH == np.arange(4)[None, :]
    consts[:, P + 4:] = part[:, None] == part[None, :]
    arrays["consts_in"] = consts
    for name, _, _ in WEIGHTS:
        w = np.asarray(inputs["L0_conv_" + name])
        if name.startswith("dec"):
            packed = deconv_blocks(w)
        elif name.endswith("ds"):
            packed = shortcut_blocks(w)
        else:
            packed = conv_blocks(w, 2 if name in ("e1b0c1", "e2b0c1") else 1)
            if name in ("e1b0c1", "e2b0c1"):
                packed = pack_sides(packed)
        arrays[name + "_in"] = np.ascontiguousarray(packed)

    nc = bacc.Bacc("TRN2", target_bir_lowering=False, num_devices=1)
    ap = {n: nc.dram_tensor(n, a.shape, F32, kind="ExternalInput").ap() for n, a in arrays.items()}
    out = nc.dram_tensor("out", (P, 8, IMAGES * 2 * 64), F32, kind="ExternalOutput").ap()
    build(nc, ap["x_in"], ap["consts_in"], [ap[n + "_in"] for n, _, _ in WEIGHTS], out)
    got = run_bass_kernel_spmd(nc, [arrays], core_ids=[0]).results[0]["out"]
    got = got.reshape(2, 2, CH, 2, 2, 2, IMAGES, 2, 8, 8)
    return np.ascontiguousarray(got.transpose(6, 2, 8, 3, 4, 0, 9, 7, 5, 1).reshape(IMAGES, CH, SIDE, SIDE))
```
